# Optimizing a Trainium2 kernel written in Bass

```python
import numpy as np
import jax
import jax.numpy as jnp

def _softmax(x, axis=-1):
    return jax.nn.softmax(x, axis=axis)

def _gelu(x):
    return jax.nn.gelu(x, approximate=True)

def _silu(x):
    return jax.nn.silu(x)

def _sigmoid(x):
    return jax.nn.sigmoid(x)

def _layernorm(x, axis=-1, eps=1e-05):
    m = jnp.mean(x, axis=axis, keepdims=True)
    v = jnp.var(x, axis=axis, keepdims=True)
    return (x - m) / jnp.sqrt(v + eps)

def _scatter_add(tgt, idx, src, axis=0):
    return tgt.at[idx].add(src)

def _segment_sum(src, seg, n):
    return jax.ops.segment_sum(src, seg, n)
kernel_name = 'mk_adj_ffn_d1_adj_r2_4bbfc5'

def setup_inputs(seed: int=0):
    np.random.seed(seed)
    _w = jnp.asarray

    def _rec_inputs():
        import jax
        import jax.numpy as jnp
        _gk = jax.random.key(seed)
        x = -8.776e-05 + 1 * jax.random.normal(jax.random.fold_in(_gk, 1), (10000, 128), jnp.float32)
        _a = jax.random.bernoulli(jax.random.fold_in(_gk, 2), 0.0016, (10000, 10000))
        _a = jnp.logical_or(_a, jnp.eye(10000, dtype=bool))
        _af = _a.astype(jnp.float32)
        _af = _af * jax.random.uniform(jax.random.fold_in(_gk, 3), (10000, 10000), jnp.float32, 0.05, 1)
        adj = _af
        return (x, adj)
    x, adj = _rec_inputs()

    def _L0_gnn_setup():
        import jax, jax.numpy as jnp
        import numpy as np
        N_USER = 10000
        N_ITEM = 10000
        HID = 128
        key = jax.random.key(seed)
        k1, k2, k3, k4, k5, k6, k7 = jax.random.split(key, 7)
        scale = 1.0 / np.sqrt(HID)
        return {'user_feat': jax.random.normal(k1, (N_USER, HID), dtype=jnp.float32), 'item_feat': jax.random.normal(k2, (N_ITEM, HID), dtype=jnp.float32), 'adj': jax.random.uniform(k3, (N_USER, N_ITEM), dtype=jnp.float32), 'W_item': jax.random.uniform(k4, (HID, HID), dtype=jnp.float32, minval=-scale, maxval=scale), 'b_item': jax.random.uniform(k5, (HID,), dtype=jnp.float32, minval=-scale, maxval=scale), 'W_user': jax.random.uniform(k6, (HID, HID), dtype=jnp.float32, minval=-scale, maxval=scale), 'b_user': jax.random.uniform(k7, (HID,), dtype=jnp.float32, minval=-scale, maxval=scale)}
    _L0_gnn_all = _L0_gnn_setup()
    _L0_gnn_in = {k: v for k, v in _L0_gnn_all.items() if k in ('item_feat', 'W_item', 'b_item', 'W_user', 'b_user')}
    del _L0_gnn_all

    def _L0_ffn_setup():
        import math
        import jax, jax.numpy as jnp
        import numpy as np
        CAPACITY_FACTOR = 1.25
        key = jax.random.key(seed)
        ks = jax.random.split(key, 5)
        B, L, D, F, E = (8, 4096, 128, 512, 8)
        h = jax.random.normal(ks[0], (B, L, D), dtype=jnp.float32)
        gate_w = jax.random.normal(ks[1], (D, E), dtype=jnp.float32) * 0.02
        gate_b = jnp.zeros((E,), dtype=jnp.float32)
        w1 = jax.random.normal(ks[2], (E, D, F), dtype=jnp.float32) * (1.0 / math.sqrt(D))
        b1 = jnp.zeros((E, F), dtype=jnp.float32)
        w2 = jax.random.normal(ks[3], (E, F, D), dtype=jnp.float32) * (1.0 / math.sqrt(F))
        b2 = jnp.zeros((E, D), dtype=jnp.float32)
        return {'h': h, 'gate_w': gate_w, 'gate_b': gate_b, 'w1': w1, 'b1': b1, 'w2': w2, 'b2': b2}
    _L0_ffn_all = _L0_ffn_setup()
    _L0_ffn_in = {k: v for k, v in _L0_ffn_all.items() if k in ('gate_w', 'gate_b', 'w1', 'b1', 'w2', 'b2')}
    del _L0_ffn_all
    return {'x': x, 'adj': adj, 'L0_gnn_item_feat': _L0_gnn_in['item_feat'], 'L0_gnn_W_item': _L0_gnn_in['W_item'], 'L0_gnn_b_item': _L0_gnn_in['b_item'], 'L0_gnn_W_user': _L0_gnn_in['W_user'], 'L0_gnn_b_user': _L0_gnn_in['b_user'], 'L0_ffn_gate_w': _L0_ffn_in['gate_w'], 'L0_ffn_gate_b': _L0_ffn_in['gate_b'], 'L0_ffn_w1': _L0_ffn_in['w1'], 'L0_ffn_b1': _L0_ffn_in['b1'], 'L0_ffn_w2': _L0_ffn_in['w2'], 'L0_ffn_b2': _L0_ffn_in['b2']}

def reference(x, adj, L0_gnn_item_feat, L0_gnn_W_item, L0_gnn_b_item, L0_gnn_W_user, L0_gnn_b_user, L0_ffn_gate_w, L0_ffn_gate_b, L0_ffn_w1, L0_ffn_b1, L0_ffn_w2, L0_ffn_b2):
    import jax
    import jax.numpy as jnp

    def _L0_gnn_ref(user_feat, item_feat, adj, W_item, b_item, W_user, b_user):
        import jax, jax.numpy as jnp
        import numpy as np
        N_USER = 10000
        N_ITEM = 10000
        HID = 128
        h = item_feat @ W_item.T + b_item
        b = user_feat @ W_user.T + b_user
        return jax.nn.relu(adj @ h + b)

    def _L0_ffn_ref(h, gate_w, gate_b, w1, b1, w2, b2):
        import math
        import jax, jax.numpy as jnp
        import numpy as np
        CAPACITY_FACTOR = 1.25
        B, L, D = h.shape
        E = gate_w.shape[1]
        T = B * L
        C = max(1, math.ceil(CAPACITY_FACTOR * T / E))
        x = h.reshape(T, D)
        logits = x @ gate_w + gate_b
        probs = jax.nn.softmax(logits, axis=-1)
        idx = jnp.argmax(probs, axis=-1)
        prb = jnp.take_along_axis(probs, idx[:, None], axis=1)[:, 0]
        one_hot = jax.nn.one_hot(idx, E, dtype=jnp.float32)
        pos = (jnp.cumsum(one_hot, axis=0) * one_hot).sum(-1).astype(jnp.int32) - 1
        kept = pos < C
        pos_safe = jnp.where(kept, pos, C)
        buf = jnp.zeros((E, C, D), dtype=h.dtype).at[idx, pos_safe].set(x, mode='drop')
        hmid = jax.nn.relu(jnp.einsum('ecd,edf->ecf', buf, w1) + b1[:, None, :])
        ybuf = jnp.einsum('ecf,efd->ecd', hmid, w2) + b2[:, None, :]
        pos_g = jnp.minimum(pos, C - 1)
        y_tok = ybuf[idx, pos_g] * (prb * kept)[:, None]
        y = y_tok.reshape(B, L, D)
        y = jnp.nan_to_num(y, nan=0.0, posinf=10000.0, neginf=-10000.0)
        return y
    x = x + _L0_gnn_ref(_layernorm(x, axis=-1), L0_gnn_item_feat, adj, L0_gnn_W_item, L0_gnn_b_item, L0_gnn_W_user, L0_gnn_b_user)
    x = x + _L0_ffn_ref(_layernorm(x, axis=-1)[None], L0_ffn_gate_w, L0_ffn_gate_b, L0_ffn_w1, L0_ffn_b1, L0_ffn_w2, L0_ffn_b2)[0]
    return x

_drawn_inputs = setup_inputs


def setup_inputs(seed=0):
    import zlib

    import numpy as np

    out = dict(_drawn_inputs(seed))
    spreads = {'L0_ffn_gate_b': (0.0, 0.1), 'L0_ffn_b1': (0.0, 0.8), 'L0_ffn_b2': (0.0, 0.797)}
    factors = {}
    for name, (base, spread) in spreads.items():
        noise = np.random.default_rng([zlib.crc32(name.encode()), seed]).standard_normal(out[name].shape)
        drawn = base * np.exp(spread * noise) if base else spread * noise
        out[name] = jnp.asarray(drawn.astype(out[name].dtype))
    for name, factor in factors.items():
        out[name] = (out[name] * factor).astype(out[name].dtype)
    return out
```

```python
from contextlib import ExitStack

import concourse.bass as bass
from concourse import mybir

ALU = mybir.AluOpType
ACT = mybir.ActivationFunctionType
AX = mybir.AxisListType
F32 = mybir.dt.float32
F32R = mybir.dt.float32r
U32 = mybir.dt.uint32

HID = 128
USERS = 10000
ITEMS = 10000

TILES = 4
TP = 125
BLOCK = TILES * TP
BLOCKS = USERS // BLOCK
FULL = ITEMS // 128
REM = ITEMS - FULL * 128
CHUNKS = FULL + 1
SIZES = [7, 6, 7, 6, 7, 6, 7, 6, 7, 6, 7, 7]
GROUPS = len(SIZES)
FIRST = [sum(SIZES[:g]) for g in range(GROUPS)]
GMAX = max(SIZES)
RAW = 3
SPLIT = 2
PER_RAW = GROUPS // RAW
HALF = GROUPS // 2
assert sum(SIZES) == CHUNKS and BLOCKS * BLOCK == USERS

EXPERTS = 8
FF = 512
FC = FF // 128
CAP = -(-5 * USERS // (4 * EXPERTS))
SLOT_P = 98
UNIT = 4 * SLOT_P
UNITS_E = -(-CAP // UNIT)
SLOTS_E = UNITS_E * UNIT
SLOTS = EXPERTS * SLOTS_E
UNITS = EXPERTS * UNITS_E
BODY = 2 * UNITS_E
REC = 132
C_GATE, C_RSTD, C_NB, C_TOK = 128, 129, 130, 131
NO_TOKEN = 16384
DROPPED = 1.0e6
EPS = 1e-5
CLIP = 1.0e4

W2 = FC * HID + FC + 1

COLS = {}
_at = 0
for _name, _n in (("ident", 128), ("tri", TP), ("rev", TILES * EXPERTS), ("tok", TILES), ("w_item", HID),
                  ("w_user", HID), ("b_item", HID), ("gate_w", EXPERTS), ("gate_b", TILES * EXPERTS),
                  ("b_user", 1)):
    COLS[_name] = (_at, _at + _n)
    _at += _n
NCONST = _at


def build(nc, adj_m, adj_r, items_t, x, consts, w1, w2, rec_d, out):
    ctx = ExitStack()
    with ctx:
        def sb(name, shape, dt=F32):
            return ctx.enter_context(nc.sbuf_tensor(name, shape, dt))

        def sem(name):
            return ctx.enter_context(nc.semaphore(name))

        cst = sb("cst", [128, NCONST])

        def const(name, rows=128):
            a, b = COLS[name]
            return cst[0:rows, a:b]

        ident = const("ident")
        h_hi = sb("h_hi", [128, CHUNKS * HID], F32R)
        h_lo = sb("h_lo", [128, CHUNKS * HID], F32R)
        raw = sb("raw", [128, RAW, GMAX * BLOCK])
        a_hi = sb("a_hi", [128, SPLIT, GMAX * BLOCK], F32R)
        a_lo = sb("a_lo", [128, SPLIT, GMAX * BLOCK], F32R)
        early = sb("early", [128, 3 * GMAX * HID])
        items = early[:, 0:2 * GMAX * HID].rearrange("p (r n) -> p r n", r=2)
        h_raw = early[:, 2 * GMAX * HID:3 * GMAX * HID]
        xb = sb("xb", [TP, TILES, HID])
        xl = sb("xl", [TP, TILES, HID])
        xlT = sb("xlT", [128, BLOCK])
        sum_a = sb("sum_a", [128, BLOCK])
        gnn = sb("gnn", [128, BLOCK])
        rec = sb("rec", [TP, TILES, REC])
        x2 = sb("x2", [TP, TILES, HID])
        x2T = sb("x2T", [128, BLOCK])
        zeros = sb("zeros", [128, 2 * REC])
        ones = sb("ones", [TP, TP])
        counts = sb("counts", [TP, EXPERTS])
        neghalf = sb("neghalf", [TP, TILES])
        quarters = sb("quarters", [TP, TILES])
        st = sb("st", [TP, TILES, 6])
        xst = sb("xst", [TP, TILES, 6])
        xw = sb("xw", [TP, TILES, 6])
        xrs = sb("xrs", [TP, TILES])
        xnb = sb("xnb", [TP, TILES])
        carrier_dve = sb("carrier_dve", [1, 1])
        w = sb("w", [TP, TILES, 6])
        carrier_pool = sb("carrier_pool", [TP, 3])
        lg = sb("lg", [TP, TILES, EXPERTS])
        lgm = sb("lgm", [TP, TILES, EXPERTS])
        mx = sb("mx", [TP, TILES])
        ex = sb("ex", [TP, TILES, EXPERTS])
        exs = sb("exs", [TP, TILES])
        wmask = sb("wmask", [TP, TILES, EXPERTS])
        best = sb("best", [TP, TILES])
        oh = sb("oh", [TP, TILES, EXPERTS])
        run = sb("run", [TP, TILES, EXPERTS])
        place = sb("place", [TP, TILES, EXPERTS])
        placed = sb("placed", [TP, TILES, EXPERTS])
        pos1 = sb("pos1", [TP, TILES])
        drop = sb("drop", [TP, TILES])
        slotf = sb("slotf", [TP, TILES])
        slot = sb("slot", [TP, TILES], U32)
        tok = sb("tok", [TP, TILES])
        wb1 = early[:, 0:2 * FF].rearrange("p (r n) -> p r n", r=2)
        wb2 = early[:, 2 * FF:2 * FF + 2 * W2].rearrange("p (r n) -> p r n", r=2)

        tail_at = [0]
        rawf = raw[:, :, :].rearrange("p r n -> p (r n)")

        def tail(rows, ring, *shape):
            n = 1
            for s in shape:
                n *= s
            a = tail_at[0]
            tail_at[0] += ring * n
            assert tail_at[0] <= RAW * GMAX * BLOCK
            v = rawf[0:rows, a:a + ring * n]
            if len(shape) == 1:
                return v.rearrange("p (r a) -> p r a", r=ring)
            return v.rearrange("p (r a b) -> p r a b", r=ring, a=shape[0])

        hm = tail(128, 2, FC, UNIT)
        recq = tail(SLOT_P, 4, 4, REC)
        x2q = tail(SLOT_P, 2, 4, HID)
        x2qT = tail(128, 2, UNIT)
        yT = tail(128, 2, UNIT)
        y = tail(SLOT_P, 2, 4, HID)
        ypos = tail(SLOT_P, 1, 4 * HID)
        yneg = xl[0:SLOT_P, :, :].rearrange("p j d -> p (j d)").unsqueeze(1)
        ymask = x2[0:SLOT_P, :, :].rearrange("p j d -> p (j d)").unsqueeze(1)
        yout = tail(SLOT_P, 2, 4, HID)
        toki = sb("toki", [SLOT_P, 4, 4], U32)

        bank = [ctx.enter_context(nc.psum_tensor(f"bank{i}", [128, 512], F32)) for i in range(8)]
        acc_a, acc_b, ps_gnn, ps_x, ps_g, ps_h0, ps_h1 = bank[:7]
        ps_logit = ps_g[0:TP, 0:TILES * EXPERTS].rearrange("p (j e) -> p j e", j=TILES)
        ps_count = bank[7][0:TP, 0:EXPERTS]
        ps_h = [ps_h0, ps_h1]
        ps_mid, ps_in, ps_y, ps_out = bank[0:4], bank[4], bank[5], bank[6]

        consts_loaded = sem("consts_loaded")
        zeros_set = sem("zeros_set")
        x1_stored = sem("x1_stored")
        scattered = sem("scattered")
        rec_free = sem("rec_free")
        set_up = sem("set_up")
        items_loaded = [sem(f"items_loaded{i}") for i in range(2)]
        h_product = sem("h_product")
        h_biased = sem("h_biased")
        h_hi_ready = sem("h_hi_ready")
        h_lo_ready = sem("h_lo_ready")
        raw_loaded = [sem(f"raw_loaded{i}") for i in range(RAW)]
        hi_ready = sem("hi_ready")
        lo_ready = sem("lo_ready")
        multiplied = sem("multiplied")
        x_loaded = sem("x_loaded")
        x_stats = sem("x_stats")
        x_norm = sem("x_norm")
        xl_ready = sem("xl_ready")
        xl_turned = sem("xl_turned")
        xlT_ready = sem("xlT_ready")
        a_taken = sem("a_taken")
        gnn_ready = sem("gnn_ready")
        gnn_turned = sem("gnn_turned")
        x1_ready = sem("x1_ready")
        stats_ready = sem("stats_ready")
        norm_ready = sem("norm_ready")
        x2_ready = sem("x2_ready")
        x2_turned = sem("x2_turned")
        x2T_ready = sem("x2T_ready")
        logits_done = sem("logits_done")
        shifted = sem("shifted")
        exp_done = sem("exp_done")
        run_ready = sem("run_ready")
        count_done = sem("count_done")
        slots_ready = sem("slots_ready")
        dve_chain = sem("dve_chain")
        pool_x_chain = sem("pool_x_chain")
        pool_x1_chain = sem("pool_x1_chain")
        weights_loaded = [sem(f"weights_loaded{i}") for i in range(2)]
        recq_loaded = [sem(f"recq_loaded{i}") for i in range(4)]
        x2q_ready = sem("x2q_ready")
        x2q_turned = sem("x2q_turned")
        x2qT_ready = sem("x2qT_ready")
        mid_done = sem("mid_done")
        hm_ready = sem("hm_ready")
        y_done = sem("y_done")
        yT_ready = sem("yT_ready")
        y_turned = sem("y_turned")
        y_ready = sem("y_ready")
        yout_ready = sem("yout_ready")
        y_gated = sem("y_gated")
        y_parts = sem("y_parts")
        toki_ready = sem("toki_ready")
        sent = [sem(f"sent{i}") for i in range(2)]

        class Chain:

            def __init__(self, eng, s, per):
                self.eng, self.s, self.per, self.n, self.base = eng, s, per, 0, 0

            def round(self, r):
                assert self.n in (0, self.per), (self.n, self.per)
                self.n, self.base = 0, r * self.per

            def did(self, ins):
                ins.then_inc(self.s, 1)
                self.n += 1

            def link(self, ins):
                self.did(ins)
                self.eng.wait_ge(self.s, self.base + self.n)

        def blocks(eng, body):
            body(0)
            with eng.Fori(1, BLOCKS) as b:
                body(b)

        def steps(eng, step):
            for k in range(BODY):
                step(0, k, k)
            with eng.Fori(1, UNITS // BODY) as i:
                for k in range(BODY):
                    step(i, k, None)
            for s in range(UNITS, UNITS + 3):
                step(s // BODY, s % BODY, s)

        def has(at, lag):
            return at is None or 0 <= at - lag < UNITS

        def group_cols(g):
            return SIZES[g] * BLOCK

        def stored_by(n):
            return n * 32 + 16

        def loads(b, g):
            extra = 1 if g % RAW == (GROUPS - 1) % RAW else 0
            return (b * (PER_RAW + extra) + g // RAW + 1 + (1 if g == GROUPS - 1 else 0)) * 16

        def wait_on_dve(dve, s, n):
            dve.wait_ge(s, n)
            nc.vector.memset(carrier_dve[:, :], 0.0)

        def wait_on_pool(pool, s, n, cell=0):
            pool.wait_ge(s, n)
            return nc.gpsimd.tensor_tensor(carrier_pool[:, cell:cell + 1], ones[:, 0:1], ones[:, 0:1], ALU.add)

        block = ctx.enter_context(nc.Block())

        @block.sync
        def _(sp):
            x_rows = x.rearrange("(r j) d -> r (j d)", j=TILES)
            out_rows = out.rearrange("(r j) d -> r (j d)", j=TILES)
            parts = ((0, 112), (112, TP))

            def load_items(g):
                if g >= 2:
                    sp.wait_ge(h_product, g - 1)
                a = FIRST[g] * 128
                b = min(a + SIZES[g] * 128, ITEMS)
                sp.dma_start(items[:, g % 2, 0:b - a], items_t[:, a:b]).then_inc(items_loaded[g % 2], 16)

            def load_x(b):
                for lo, hi in parts:
                    sp.dma_start(xb[lo:hi, :, :].rearrange("p j d -> p (j d)"),
                                 x_rows[bass.ds(b * TP + lo, hi - lo), :]).then_inc(x_loaded, 16)

            def body(b):
                first = isinstance(b, int)
                for g in range(GROUPS):
                    if first:
                        load_items(g)
                    if not first or g >= RAW:
                        sp.wait_ge(lo_ready, b * GROUPS + g - RAW + 1)
                    last = g == GROUPS - 1
                    n = (SIZES[g] - last) * BLOCK
                    a = FIRST[g] * BLOCK
                    adj_b = adj_m[b] if first else adj_m[bass.ds(b, 1), :, :].rearrange("o p n -> (o p) n")
                    sp.dma_start(raw[:, g % RAW, 0:n], adj_b[:, a:a + n],
                                 max_dma_last_dim=16384).then_inc(raw_loaded[g % RAW], 16)
                    if last:
                        rem_b = adj_r[b] if first else adj_r[bass.ds(b, 1), :, :].rearrange("o p n -> (o p) n")
                        sp.dma_start(raw[0:REM, g % RAW, n:n + BLOCK], rem_b).then_inc(raw_loaded[g % RAW], 16)
                    if first and g == 3:
                        load_x(b)
                    if first and g == GROUPS - 1:
                        sp.wait_ge(x1_stored, stored_by(0))
                    if not first and g == 6:
                        sp.wait_ge(x1_ready, b)
                        load_x(b)
                        for lo, hi in parts:
                            sp.dma_start(out_rows[bass.ds((b - 1) * TP + lo, hi - lo), :],
                                         rec[lo:hi, :, 0:HID]).then_inc(x1_stored, 16)

            sp.dma_start(cst[:, :], consts).then_inc(consts_loaded, 16)
            blocks(sp, body)
            sp.wait_ge(x1_ready, BLOCKS)
            for lo, hi in parts:
                sp.dma_start(out_rows[(BLOCKS - 1) * TP + lo:(BLOCKS - 1) * TP + hi, :],
                             rec[lo:hi, :, 0:HID]).then_inc(x1_stored, 16)

            def load_weights(e, slot_, wait):
                if wait:
                    sp.wait_ge(yT_ready, (e - 1) * UNITS_E)
                w1_e = w1[bass.ds(e, 1), :, :].rearrange("o p n -> (o p) n")
                w2_e = w2[bass.ds(e, 1), :, :].rearrange("o p n -> (o p) n")
                sp.dma_start(wb1[:, slot_, :], w1_e).then_inc(weights_loaded[slot_], 16)
                sp.dma_start(wb2[:, slot_, :], w2_e).then_inc(weights_loaded[slot_], 16)

            rec_units = rec_d.rearrange("(r j) c -> r (j c)", j=4)

            def load_rec(q, k, wait):
                if wait:
                    sp.wait_ge(yout_ready, q - 3)
                sp.dma_start(recq[:, k % 4, :, :].rearrange("p j c -> p (j c)"),
                             rec_units[bass.ds(q * SLOT_P, SLOT_P), :]).then_inc(recq_loaded[k % 4], 16)

            sp.wait_ge(h_lo_ready, GROUPS)
            load_weights(0, 0, False)
            load_weights(1, 1, False)
            sp.wait_ge(rec_free, BLOCKS + 1)
            for k in range(BODY):
                load_rec(k, k, k >= 4)
            with sp.Fori(1, UNITS // BODY) as i:
                for k in range(BODY):
                    if k % UNITS_E == 2:
                        load_weights(i * 2 + k // UNITS_E, k // UNITS_E, True)
                    load_rec(i * BODY + k, k, True)
            for k in range(2):
                sp.wait_ge(sent[k], UNITS // 2 * 64)

        @block.scalar
        def _(act):
            act.wait_ge(zeros_set, 1)
            act.dma_start(rec_d.rearrange("(p a r) c -> p a (r c)", p=128, r=2),
                          zeros[:, :].unsqueeze(1).broadcast_to([128, SLOTS // 256, 2 * REC])
                          ).then_inc(x1_stored, 16)
            act.wait_ge(consts_loaded, 16)

            def h_high(g):
                act.wait_ge(h_biased, g + 1)
                a, n = FIRST[g] * HID, SIZES[g] * HID
                m = n - HID if g == GROUPS - 1 else n
                last = nc.scalar.copy(h_hi[:, a:a + m], h_raw[:, 0:m])
                if m < n:
                    last = nc.scalar.copy(h_hi[0:REM, a + m:a + n], h_raw[0:REM, m:n])
                last.then_inc(h_hi_ready, 1)

            def high(b, g):
                act.wait_ge(raw_loaded[g % RAW], loads(b, g))
                if not isinstance(b, int) or g >= SPLIT:
                    act.wait_ge(multiplied, b * GROUPS + g - SPLIT + 1)
                m = group_cols(g)
                nc.scalar.copy(a_hi[:, g % SPLIT, 0:m], raw[:, g % RAW, 0:m]).then_inc(hi_ready, 1)

            def take_a(b):
                act.wait_ge(multiplied, b * GROUPS + HALF)
                if not isinstance(b, int):
                    act.wait_ge(gnn_ready, b)
                nc.scalar.activation(sum_a[:, :], acc_a[:, 0:BLOCK], ACT.Identity,
                                     bias=const("b_user")).then_inc(a_taken, 1)

            def normalize_x(b):
                act.wait_ge(x_norm, b + 1)
                if not isinstance(b, int):
                    act.wait_ge(xl_turned, b)
                for j in range(TILES):
                    last = nc.scalar.activation(xl[:, j, :], xb[:, j, :], ACT.Identity,
                                                scale=xrs[:, j:j + 1], bias=xnb[:, j:j + 1])
                last.then_inc(xl_ready, 1)

            def take_xl(b):
                act.wait_ge(xl_turned, b + 1)
                if not isinstance(b, int):
                    act.wait_ge(multiplied, b * GROUPS)
                nc.scalar.copy(xlT[:, :], ps_x[:, 0:BLOCK]).then_inc(xlT_ready, 1)

            def normalize_x1(n):
                act.wait_ge(norm_ready, n + 1)
                for j in range(TILES):
                    last = nc.scalar.activation(x2[:, j, :], rec[:, j, 0:HID], ACT.Identity,
                                                scale=rec[:, j, C_RSTD:C_RSTD + 1],
                                                bias=rec[:, j, C_NB:C_NB + 1])
                last.then_inc(x2_ready, 1)

            def take_x2(n):
                act.wait_ge(x2_turned, n + 1)
                nc.scalar.copy(x2T[:, :], ps_x[:, 0:BLOCK]).then_inc(x2T_ready, 1)

            def exps(n):
                act.wait_ge(shifted, n + 1)
                nc.scalar.activation(ex[:, :, :], lgm[:, :, :], ACT.Exp).then_inc(exp_done, 1)

            def body(b):
                first = isinstance(b, int)
                for g in range(GROUPS):
                    if first:
                        h_high(g)
                    high(b, g)
                    if not first:
                        {5: normalize_x1, 7: take_x2, 10: exps}.get(g, lambda n: None)(b - 1)
                    {8: normalize_x, 9: take_a, 10: take_xl}.get(g, lambda b: None)(b)

            blocks(act, body)
            normalize_x1(BLOCKS - 1)
            take_x2(BLOCKS - 1)
            exps(BLOCKS - 1)

            def bias_of(k, lag, col):
                return wb2[:, (k - lag) // UNITS_E % 2, FC * HID + col:FC * HID + col + 1]

            def step(i, k, at):
                s = i * BODY + k
                if has(at, 0):
                    act.wait_ge(x2q_turned, s + 1)
                    if at is None or at >= 2:
                        act.wait_ge(mid_done, (s - 1) * FC)
                    nc.scalar.copy(x2qT[:, k % 2, :], ps_in[:, 0:UNIT]).then_inc(x2qT_ready, 1)
                if has(at, 1):
                    if at is None or at - 1 >= 2:
                        act.wait_ge(y_done, s - 2)
                    for f in range(FC):
                        act.wait_ge(mid_done, (s - 1) * FC + f + 1)
                        nc.scalar.activation(hm[:, (k - 1) % 2, f, :], ps_mid[f][:, 0:UNIT], ACT.Relu,
                                             bias=bias_of(k, 1, f)).then_inc(hm_ready, 1)
                if has(at, 2):
                    act.wait_ge(y_done, s - 1)
                    if at is None or at - 2 >= 2:
                        act.wait_ge(y_turned, s - 3)
                    nc.scalar.activation(yT[:, k % 2, :], ps_y[:, 0:UNIT], ACT.Identity,
                                         bias=bias_of(k, 2, FC)).then_inc(yT_ready, 1)

            steps(act, step)

        @block.vector
        def _(dve):
            v = nc.vector
            chain = Chain(dve, dve_chain, 18)
            rev = const("rev", TP).rearrange("p (j e) -> p j e", j=TILES)
            gate_b = const("gate_b", TP).rearrange("p (j e) -> p j e", j=TILES)

            def each(t):
                return t[:, :].unsqueeze(2).broadcast_to([TP, TILES, EXPERTS])

            def h_bias(g):
                dve.wait_ge(h_product, g + 1)
                if g >= 1:
                    dve.wait_ge(h_lo_ready, g)
                n = SIZES[g]
                m = n - 1 if g == GROUPS - 1 else n
                for c0, c1 in ((0, 4), (4, m)):
                    last = v.tensor_tensor(
                        h_raw[:, c0 * HID:c1 * HID].rearrange("p (c d) -> p c d", d=HID),
                        ps_h[c0 // 4][:, 0:(c1 - c0) * HID].rearrange("p (c d) -> p c d", d=HID),
                        const("b_item").unsqueeze(1).broadcast_to([128, c1 - c0, HID]), ALU.add)
                if m < n:
                    last = v.tensor_tensor(h_raw[0:REM, m * HID:n * HID],
                                           ps_h[1][0:REM, (m - 4) * HID:(n - 4) * HID],
                                           const("b_item", REM), ALU.add)
                last.then_inc(h_biased, 1)

            def h_low(g):
                dve.wait_ge(h_hi_ready, g + 1)
                a, n = FIRST[g] * HID, SIZES[g] * HID
                m = n - HID if g == GROUPS - 1 else n
                last = v.tensor_tensor(h_lo[:, a:a + m], h_raw[:, 0:m], h_hi[:, a:a + m].bitcast(F32), ALU.subtract)
                if m < n:
                    last = v.tensor_tensor(h_lo[0:REM, a + m:a + n], h_raw[0:REM, m:n],
                                           h_hi[0:REM, a + m:a + n].bitcast(F32), ALU.subtract)
                last.then_inc(h_lo_ready, 1)

            def low(b, g):
                dve.wait_ge(hi_ready, b * GROUPS + g + 1)
                m = group_cols(g)
                v.tensor_tensor(a_lo[:, g % SPLIT, 0:m], raw[:, g % RAW, 0:m],
                                a_hi[:, g % SPLIT, 0:m].bitcast(F32), ALU.subtract).then_inc(lo_ready, 1)

            def x_statistics(b):
                dve.wait_ge(x_loaded, 32 * (b + 1))
                if not isinstance(b, int):
                    dve.wait_ge(x_norm, b)
                for j in range(TILES):
                    last = v.bn_stats(xst[:, j, :], xb[:, j, :])
                last.then_inc(x_stats, 1)

            def sum_gnn(n):
                dve.wait_ge(multiplied, (n + 1) * GROUPS)
                dve.wait_ge(a_taken, n + 1)
                v.tensor_tensor(gnn[:, :], acc_b[:, 0:BLOCK], sum_a[:, :], ALU.add).then_inc(gnn_ready, 1)

            def add_x(n):
                chain.round(n)
                dve.wait_ge(gnn_turned, n + 1)
                dve.wait_ge(x1_stored, stored_by(n))
                dve.wait_ge(rec_free, n + 1)
                v.scalar_tensor_tensor(out=rec[:, :, 0:HID],
                                       in0=ps_gnn[0:TP, :].rearrange("p (j d) -> p j d", j=TILES), scalar=0.0,
                                       in1=xb[:, :, :], op0=ALU.max, op1=ALU.add).then_inc(x1_ready, 1)
                dve.wait_ge(x1_ready, n + 1)
                for j in range(TILES):
                    last = v.bn_stats(st[:, j, :], rec[:, j, 0:HID])
                last.then_inc(stats_ready, 1)

            def choose(n):
                dve.wait_ge(logits_done, n + 1)
                chain.link(v.tensor_tensor(lg[:, :, :], ps_logit, gate_b, ALU.add))
                chain.link(v.tensor_reduce(mx[:, :], lg[:, :, :], AX.X, ALU.max))
                v.tensor_tensor(lgm[:, :, :], lg[:, :, :], each(mx), ALU.subtract).then_inc(shifted, 1)
                dve.wait_ge(shifted, n + 1)
                chain.link(v.scalar_tensor_tensor(out=wmask[:, :, :], in0=lgm[:, :, :], scalar=0.0, in1=rev,
                                                  op0=ALU.is_ge, op1=ALU.mult))
                chain.link(v.tensor_reduce(best[:, :], wmask[:, :, :], AX.X, ALU.max))
                chain.link(v.tensor_tensor(oh[:, :, :], rev, each(best), ALU.is_equal))
                chain.did(v.tensor_copy(run[:, 0, :], oh[:, 0, :]))
                chain.link(v.tensor_tensor(run[:, 1, :], oh[:, 0, :], oh[:, 1, :], ALU.add))
                chain.link(v.tensor_tensor(run[:, 2, :], run[:, 1, :], oh[:, 2, :], ALU.add))
                v.tensor_tensor(run[:, 3, :], run[:, 2, :], oh[:, 3, :], ALU.add).then_inc(run_ready, 1)

            def assign(n):
                dve.wait_ge(count_done, n + 1)
                dve.wait_ge(run_ready, n + 1)
                chain.link(v.tensor_tensor(place[:, :, :], run[:, :, :],
                                           ps_count.unsqueeze(1).broadcast_to([TP, TILES, EXPERTS]), ALU.add))
                chain.link(v.tensor_tensor(placed[:, :, :], place[:, :, :], oh[:, :, :], ALU.mult))
                chain.link(v.tensor_reduce(pos1[:, :], placed[:, :, :], AX.X, ALU.add))
                chain.did(v.tensor_scalar(drop[:, :], pos1[:, :], float(CAP), DROPPED, ALU.is_gt, ALU.mult))
                chain.did(v.scalar_tensor_tensor(out=slotf[:, :], in0=best[:, :], scalar=-float(SLOTS_E),
                                                 in1=pos1[:, :], op0=ALU.mult, op1=ALU.add))
                chain.did(v.tensor_tensor(counts[:, :], counts[:, :], run[:, 3, :], ALU.add))
                dve.wait_ge(exp_done, n + 1)
                chain.did(v.tensor_reduce(exs[:, :], ex[:, :, :], AX.X, ALU.add))
                chain.link(v.tensor_copy(rec[:, :, C_TOK:C_TOK + 1], tok[:, :].unsqueeze(2)))
                chain.did(v.reciprocal(rec[:, :, C_GATE:C_GATE + 1], exs[:, :].unsqueeze(2)))
                chain.did(v.tensor_scalar(tok[:, :], tok[:, :], float(BLOCK), None, ALU.add))
                v.scalar_tensor_tensor(out=slot[:, :], in0=slotf[:, :], scalar=float(SLOTS - 1),
                                       in1=drop[:, :], op0=ALU.add, op1=ALU.add).then_inc(slots_ready, 1)

            def body(b):
                first = isinstance(b, int)
                for g in range(GROUPS):
                    if first:
                        h_bias(g)
                        h_low(g)
                    low(b, g)
                    if not first:
                        {1: sum_gnn, 3: add_x, 9: choose, 11: assign}.get(g, lambda n: None)(b - 1)
                    if g == 6:
                        x_statistics(b)

            v.memset(zeros[:, :], 0.0).then_inc(zeros_set, 1)
            v.memset(rec[:, :, :], 0.0).then_inc(rec_free, 1)
            v.memset(ones[:, :], 1.0).then_inc(set_up, 1)
            v.memset(counts[:, :], 0.0).then_inc(set_up, 1)
            v.memset(neghalf[:, :], -0.5).then_inc(set_up, 1)
            v.memset(quarters[:, :], 0.25).then_inc(set_up, 1)
            dve.wait_ge(consts_loaded, 16)
            v.tensor_copy(tok[:, :], const("tok", TP)).then_inc(set_up, 1)
            dve.wait_ge(set_up, 5)
            blocks(dve, body)
            for stage in (sum_gnn, add_x, choose, assign):
                stage(BLOCKS - 1)

            def step(i, k, at):
                s = i * BODY + k
                if has(at, 0):
                    r = k % 4
                    dve.wait_ge(recq_loaded[r], (i * (BODY // 4) + k // 4 + 1) * 16)
                    if at is None or at >= 2:
                        dve.wait_ge(x2q_turned, s - 1)
                    for j in range(4):
                        last = v.tensor_scalar(x2q[:, k % 2, j, :], recq[:, r, j, 0:HID],
                                               recq[:, r, j, C_RSTD:C_RSTD + 1], recq[:, r, j, C_NB:C_NB + 1],
                                               ALU.mult, ALU.add)
                    last.then_inc(x2q_ready, 1)
                    if at is None or at >= 4:
                        dve.wait_ge(sent[k % 2], (i * (BODY // 2) + k // 2 - 1) * 64)
                    v.tensor_scalar(toki[:, r, :].unsqueeze(2), recq[:, r, :, C_TOK:C_TOK + 1],
                                    float(NO_TOKEN), None, ALU.add).then_inc(toki_ready, 1)
                if has(at, 3):
                    u, r = (k - 3) % 2, (k - 3) % 4
                    dve.wait_ge(y_turned, s - 2)
                    if at is None or at - 3 >= 2:
                        dve.wait_ge(yout_ready, s - 4)
                    yf = y[:, u, :, :].rearrange("p j d -> p (j d)")
                    v.tensor_tensor(y[:, u, :, :], ps_out[0:SLOT_P, :].rearrange("p (j d) -> p j d", j=4),
                                    recq[:, r, :, C_GATE:C_GATE + 1].broadcast_to([SLOT_P, 4, HID]),
                                    ALU.mult).then_inc(y_gated, 1)
                    dve.wait_ge(y_gated, s - 2)
                    v.tensor_scalar(ypos[:, 0, :], yf, 0.0, CLIP, ALU.max, ALU.min)
                    v.tensor_scalar(yneg[:, 0, :], yf, 0.0, -CLIP, ALU.min, ALU.max)
                    v.tensor_scalar(ymask[:, 0, :].bitcast(U32), yf, 0.0, 0.0, ALU.mult,
                                    ALU.not_equal).then_inc(y_parts, 1)
                    dve.wait_ge(y_parts, (s - 3) * 2 + 1)
                    v.tensor_tensor(ypos[:, 0, :], ypos[:, 0, :], yneg[:, 0, :], ALU.add).then_inc(y_parts, 1)
                    wait_on_dve(dve, y_parts, (s - 2) * 2)
                    v.copy_predicated(yf, ymask[:, 0, :].bitcast(U32), ypos[:, 0, :]).then_inc(y_ready, 1)

            steps(dve, step)

        @block.gpsimd
        def _(pool):
            p = nc.gpsimd
            def norm(sums, w, rstd, nb, chain, done):
                def cell(k):
                    return w[:, :, k:k + 1]

                total, diff, sq, diff2, quarter, var = map(cell, range(6))
                chain.did(p.tensor_tensor(total, sums[:, :, 1:2], sums[:, :, 4:5], ALU.add))
                chain.did(p.tensor_tensor(diff, sums[:, :, 1:2], sums[:, :, 4:5], ALU.subtract))
                chain.link(p.tensor_tensor(sq, sums[:, :, 2:3], sums[:, :, 5:6], ALU.add))
                chain.did(p.tensor_tensor(diff2, diff, diff, ALU.mult))
                chain.did(p.tensor_scalar(total, total, -0.5, None, ALU.mult))
                chain.link(p.tensor_scalar(sq, sq, 1.0 / HID, EPS, ALU.mult, ALU.add))
                chain.link(p.tensor_tensor(quarter, diff2, quarters[:, :].unsqueeze(2), ALU.mult))
                chain.link(p.tensor_tensor(var, quarter, sq, ALU.add))
                chain.link(p.tensor_tensor(rstd, var, neghalf[:, :].unsqueeze(2), ALU.pow))
                p.tensor_tensor(nb, total, rstd, ALU.mult).then_inc(done, 1)

            x_chain = Chain(pool, pool_x_chain, 9)
            x1_chain = Chain(pool, pool_x1_chain, 9)

            def norm_x(b):
                x_chain.round(b)
                if not isinstance(b, int):
                    pool.wait_ge(xl_ready, b)
                pool.wait_ge(x_stats, b + 1)
                norm(xst, xw, xrs[:, :].unsqueeze(2), xnb[:, :].unsqueeze(2), x_chain, x_norm)

            def norm_x1(n):
                x1_chain.round(n)
                pool.wait_ge(stats_ready, n + 1)
                norm(st, w, rec[:, :, C_RSTD:C_RSTD + 1], rec[:, :, C_NB:C_NB + 1], x1_chain, norm_ready)

            def scatter(n):
                wait_on_pool(pool, slots_ready, n + 1)
                for j in range(TILES):
                    p.indirect_dma_start(rec_d, bass.IndirectOffsetOnAxis(ap=slot[:, j:j + 1], axis=0),
                                         rec[:, j, :], None, bounds_check=SLOTS - 1,
                                         oob_is_err=False).then_inc(scattered, 16)
                wait_on_pool(pool, scattered, (n + 1) * (TILES * 16), 1).then_inc(rec_free, 1)

            pool.wait_ge(set_up, 5)
            norm_x(0)
            pool.wait_ge(x1_stored, stored_by(0))
            with pool.Fori(1, BLOCKS) as b:
                norm_x1(b - 1)
                norm_x(b)
                scatter(b - 1)
            norm_x1(BLOCKS - 1)
            scatter(BLOCKS - 1)
            pool.wait_ge(x1_stored, stored_by(BLOCKS))

            def step(i, k, at):
                s = i * BODY + k
                if has(at, 3):
                    u, r = (k - 3) % 2, (k - 3) % 4
                    pool.wait_ge(y_ready, s - 2)
                    if at is None or at - 3 >= 2:
                        pool.wait_ge(sent[u], (i * (BODY // 2) + (k - 3) // 2) * 64)
                    p.tensor_tensor(yout[:, u, :, :], y[:, u, :, :], recq[:, r, :, 0:HID],
                                    ALU.add).then_inc(yout_ready, 1)
                    pool.wait_ge(toki_ready, s - 2)
                    wait_on_pool(pool, yout_ready, s - 2, 2)
                    for j in range(4):
                        p.indirect_dma_start(out, bass.IndirectOffsetOnAxis(ap=toki[:, r, j:j + 1], axis=0),
                                             yout[:, u, j, :], None, bounds_check=USERS - 1,
                                             oob_is_err=False).then_inc(sent[u], 16)

            steps(pool, step)

        @block.tensor
        def _(pe):
            def h_chunks(g):
                pe.wait_ge(items_loaded[g % 2], 16 * (g // 2 + 1))
                if g >= 1:
                    pe.wait_ge(h_biased, g)
                for c in range(SIZES[g]):
                    m = REM if FIRST[g] + c == FULL else 128
                    last = nc.tensor.matmul(ps_h[c // 4][0:m, (c % 4) * HID:(c % 4 + 1) * HID],
                                            items[:, g % 2, c * 128:c * 128 + m], const("w_item"),
                                            start=True, stop=True)
                last.then_inc(h_product, 1)

            def group(b, g):
                first = isinstance(b, int)
                acc = (acc_a if g < HALF else acc_b)[:, 0:BLOCK]
                if first:
                    pe.wait_ge(h_hi_ready, g + 1)
                    pe.wait_ge(h_lo_ready, g + 1)
                elif g == 0:
                    pe.wait_ge(a_taken, b)
                elif g == HALF:
                    pe.wait_ge(gnn_ready, b)
                pe.wait_ge(hi_ready, b * GROUPS + g + 1)
                for part in range(2):
                    if part:
                        pe.wait_ge(lo_ready, b * GROUPS + g + 1)
                    for c in range(SIZES[g]):
                        m = REM if FIRST[g] + c == FULL else 128
                        k = FIRST[g] + c
                        opens = g in (0, HALF) and c == 0 and part == 0
                        closes = g in (HALF - 1, GROUPS - 1) and c == SIZES[g] - 1 and part == 1
                        h_high, h_low = h_hi[0:m, k * HID:(k + 1) * HID], h_lo[0:m, k * HID:(k + 1) * HID]
                        a = (a_lo if part else a_hi)[0:m, g % SPLIT, c * BLOCK:(c + 1) * BLOCK]
                        last = nc.tensor.matmul(acc, h_high, a, start=opens, stop=closes)
                        if not part:
                            nc.tensor.matmul(acc, h_low, a, start=False, stop=False)
                last.then_inc(multiplied, 1)

            def turn_x(b):
                pe.wait_ge(xl_ready, b + 1)
                if not isinstance(b, int):
                    pe.wait_ge(x2T_ready, b)
                for j in range(TILES):
                    last = nc.tensor.transpose(ps_x[:, j * TP:(j + 1) * TP], xl[:, j, :], ident[0:TP, 0:TP])
                last.then_inc(xl_turned, 1)

            def users(b):
                pe.wait_ge(xlT_ready, b + 1)
                nc.tensor.matmul(acc_b[:, 0:BLOCK], const("w_user"), xlT[:, :], start=False, stop=False)

            def turn_gnn(n):
                pe.wait_ge(gnn_ready, n + 1)
                for j in range(TILES):
                    last = nc.tensor.transpose(ps_gnn[0:TP, j * HID:(j + 1) * HID], gnn[:, j * TP:(j + 1) * TP],
                                               ident)
                last.then_inc(gnn_turned, 1)

            def turn_x2(n):
                pe.wait_ge(x2_ready, n + 1)
                pe.wait_ge(xlT_ready, n + 1)
                for j in range(TILES):
                    last = nc.tensor.transpose(ps_x[:, j * TP:(j + 1) * TP], x2[:, j, :], ident[0:TP, 0:TP])
                last.then_inc(x2_turned, 1)

            def logits(n):
                pe.wait_ge(x2T_ready, n + 1)
                for j in range(TILES):
                    last = nc.tensor.matmul(ps_logit[:, j, :], x2T[:, j * TP:(j + 1) * TP], const("gate_w"),
                                            start=True, stop=True)
                last.then_inc(logits_done, 1)

            def count(n):
                pe.wait_ge(run_ready, n + 1)
                nc.tensor.matmul(ps_count, const("tri", TP), run[:, 3, :], start=True, stop=False)
                nc.tensor.matmul(ps_count, ones[:, :], counts[:, :], start=False, stop=True).then_inc(count_done, 1)

            def body(b):
                first = isinstance(b, int)
                for g in range(GROUPS):
                    if first:
                        h_chunks(g)
                    group(b, g)
                    if not first:
                        {1: turn_gnn, 5: turn_x2, 7: logits, 9: count}.get(g, lambda n: None)(b - 1)
                    {8: turn_x, 10: users}.get(g, lambda b: None)(b)

            pe.wait_ge(consts_loaded, 16)
            pe.wait_ge(set_up, 5)
            blocks(pe, body)
            for stage in (turn_gnn, turn_x2, logits, count):
                stage(BLOCKS - 1)

            def step(i, k, at):
                s = i * BODY + k
                if has(at, 0):
                    pe.wait_ge(x2q_ready, s + 1)
                    if at is None or at >= 1:
                        pe.wait_ge(x2qT_ready, s)
                    for j in range(4):
                        last = nc.tensor.transpose(ps_in[:, j * SLOT_P:(j + 1) * SLOT_P], x2q[:, k % 2, j, :],
                                                   ident[0:SLOT_P, 0:SLOT_P])
                    last.then_inc(x2q_turned, 1)
                if has(at, 3):
                    pe.wait_ge(yT_ready, s - 2)
                    if at is None or at >= 4:
                        pe.wait_ge(y_gated, s - 3)
                    for j in range(4):
                        last = nc.tensor.transpose(ps_out[0:SLOT_P, j * HID:(j + 1) * HID],
                                                   yT[:, (k - 3) % 2, j * SLOT_P:(j + 1) * SLOT_P], ident)
                    last.then_inc(y_turned, 1)
                if has(at, 1):
                    w = (k - 1) // UNITS_E % 2
                    pe.wait_ge(weights_loaded[w], (i + (k - 1) // BODY + 1) * 32)
                    pe.wait_ge(x2qT_ready, s)
                    for f in range(FC):
                        if at is None or at >= 2:
                            pe.wait_ge(hm_ready, (s - 2) * FC + f + 1)
                        nc.tensor.matmul(ps_mid[f][:, 0:UNIT], wb1[:, w, f * 128:(f + 1) * 128],
                                         x2qT[:, (k - 1) % 2, :], start=True, stop=True).then_inc(mid_done, 1)
                if has(at, 2):
                    w = (k - 2) // UNITS_E % 2
                    pe.wait_ge(hm_ready, (s - 1) * FC)
                    if at is None or at >= 3:
                        pe.wait_ge(yT_ready, s - 2)
                    for f in range(FC):
                        last = nc.tensor.matmul(ps_y[:, 0:UNIT], wb2[:, w, f * HID:(f + 1) * HID],
                                                hm[:, (k - 2) % 2, f, :], start=(f == 0), stop=(f == FC - 1))
                    last.then_inc(y_done, 1)

            steps(pe, step)


def kernel(x, adj, L0_gnn_item_feat, L0_gnn_W_item, L0_gnn_b_item, L0_gnn_W_user, L0_gnn_b_user,
           L0_ffn_gate_w, L0_ffn_gate_b, L0_ffn_w1, L0_ffn_b1, L0_ffn_w2, L0_ffn_b2):
    import numpy as np
    import concourse.bacc as bacc
    from concourse.bass_utils import run_bass_kernel_spmd

    adj_t = np.asarray(adj).reshape(BLOCKS, TP, TILES, ITEMS).transpose(0, 3, 2, 1)
    adj_m = np.ascontiguousarray(
        adj_t[:, :FULL * 128].reshape(BLOCKS, FULL, 128, TILES, TP).transpose(0, 2, 1, 3, 4)
    ).reshape(BLOCKS, 128, FULL * BLOCK)
    adj_r = np.ascontiguousarray(adj_t[:, FULL * 128:]).reshape(BLOCKS, REM, BLOCK)

    consts = np.zeros((128, NCONST), np.float32)

    def put(name, a):
        lo, hi = COLS[name]
        consts[:a.shape[0], lo:hi] = a

    q = np.arange(TP)
    put("ident", np.eye(128, dtype=np.float32))
    put("tri", (q[:, None] < q[None, :]).astype(np.float32))
    put("rev", np.tile((EXPERTS - np.arange(EXPERTS)).astype(np.float32), (TP, TILES)))
    put("tok", (q[:, None] * TILES + np.arange(TILES)[None, :] - NO_TOKEN).astype(np.float32))
    put("w_item", np.asarray(L0_gnn_W_item).T)
    put("w_user", np.asarray(L0_gnn_W_user).T)
    put("b_item", np.tile(np.asarray(L0_gnn_b_item), (128, 1)))
    put("gate_w", np.asarray(L0_ffn_gate_w))
    put("gate_b", np.tile(np.asarray(L0_ffn_gate_b), (TP, TILES)))
    put("b_user", np.asarray(L0_gnn_b_user).reshape(HID, 1))

    arrays = {
        "adj_m": adj_m,
        "adj_r": adj_r,
        "items_t": np.ascontiguousarray(np.asarray(L0_gnn_item_feat).T),
        "x": np.ascontiguousarray(np.asarray(x)),
        "consts": consts,
        "w1": np.ascontiguousarray(np.asarray(L0_ffn_w1)),
        "w2": np.concatenate([
            np.asarray(L0_ffn_w2).reshape(EXPERTS, FC, 128, HID).transpose(0, 2, 1, 3).reshape(EXPERTS, 128, FC * HID),
            np.asarray(L0_ffn_b1).reshape(EXPERTS, FC, 128).transpose(0, 2, 1),
            np.asarray(L0_ffn_b2).reshape(EXPERTS, HID, 1)], axis=2),
    }
    nc = bacc.Bacc("TRN2", target_bir_lowering=False, num_devices=1)
    aps = [nc.dram_tensor(name, a.shape, mybir.dt.from_np(a.dtype), kind="ExternalInput").ap()
           for name, a in arrays.items()]
    rec_d = nc.dram_tensor("records", (SLOTS, REC), F32, kind="Internal").ap()
    out = nc.dram_tensor("out", (USERS, HID), F32, kind="ExternalOutput").ap()
    build(nc, *aps, rec_d, out)
    r = run_bass_kernel_spmd(nc, [arrays], core_ids=[0])
    return r.results[0]["out"]
```

```python
from contextlib import ExitStack

import concourse.bass as bass
from concourse import mybir

ALU = mybir.AluOpType
ACT = mybir.ActivationFunctionType
AX = mybir.AxisListType
F32 = mybir.dt.float32
F32R = mybir.dt.float32r
U32 = mybir.dt.uint32

HID = 128
USERS = 10000
ITEMS = 10000

TILES = 4
TP = 125
BLOCK = TILES * TP
BLOCKS = USERS // BLOCK
FULL = ITEMS // 128
REM = ITEMS - FULL * 128
CHUNKS = FULL + 1
SIZES = [4] * 19 + [3]
GROUPS = len(SIZES)
FIRST = [sum(SIZES[:g]) for g in range(GROUPS)]
GMAX = max(SIZES)
RAW = 5
HI_RING = 4
LO_RING = 2
PER_RAW = GROUPS // RAW
HALF = GROUPS // 2
assert sum(SIZES) == CHUNKS and GMAX <= 4 and BLOCKS * BLOCK == USERS

EXPERTS = 8
FF = 512
FC = FF // 128
CAP = -(-5 * USERS // (4 * EXPERTS))
SLOT_P = 98
UNIT = 4 * SLOT_P
UNITS_E = -(-CAP // UNIT)
SLOTS_E = UNITS_E * UNIT
SLOTS = EXPERTS * SLOTS_E
UNITS = EXPERTS * UNITS_E
RUN = 14
RUNS = SLOTS_E // RUN
EDGE = EXPERTS * RUN
assert SLOTS_E % RUN == 0 and max(RUNS, EDGE) <= TP
BODY = 2 * UNITS_E
LAG_IN, LAG_MID, LAG_Y, LAG_OUT = 1, 2, 3, 5
REC = 132
C_GATE, C_RSTD, C_NB, C_TOK = 128, 129, 130, 131
NO_TOKEN = 16384
BEYOND = 1.0e6
EPS = 1e-5
CLIP = 1.0e4

W2 = FC * HID + FC + 1

COLS = {}
_at = 0
for _name, _n in (("ident", 128), ("tri", TP), ("rev", TILES * EXPERTS), ("tok", 2 * TILES), ("w_item", HID),
                  ("w_user", HID), ("b_item", HID), ("gate_w", EXPERTS), ("gate_b", TILES * EXPERTS),
                  ("run_at", 1), ("run_no", EXPERTS), ("edge_of", EXPERTS),
                  ("starts", RUNS), ("edge_no", 1), ("edge_at", 1), ("b_user", 1)):
    COLS[_name] = (_at, _at + _n)
    _at += _n
NCONST = _at


def build(nc, adj_m, adj_r, items_t, x, consts, w1, w2, rec_d, out):
    ctx = ExitStack()
    with ctx:
        def sb(name, shape, dt=F32):
            return ctx.enter_context(nc.sbuf_tensor(name, shape, dt))

        def sem(name):
            return ctx.enter_context(nc.semaphore(name))

        cst = sb("cst", [128, NCONST])

        def const(name, rows=128):
            a, b = COLS[name]
            return cst[0:rows, a:b]

        ident = const("ident")
        h_hi = sb("h_hi", [128, CHUNKS * HID], F32R)
        h_lo = sb("h_lo", [128, CHUNKS * HID], F32R)
        raw = sb("raw", [128, RAW, GMAX * BLOCK])
        a_hi = sb("a_hi", [128, HI_RING, GMAX * BLOCK], F32R)
        a_lo = sb("a_lo", [128, LO_RING, GMAX * BLOCK], F32R)
        early = sb("early", [128, max(3 * GMAX * HID, 2 * FF + 2 * W2)])
        items = early[:, 0:2 * GMAX * HID].rearrange("p (r n) -> p r n", r=2)
        zeros = early[:, 0:RUN * REC]
        h_raw = early[:, 2 * GMAX * HID:3 * GMAX * HID]
        xb = sb("xb", [TP, TILES, HID])
        xl = sb("xl", [TP, TILES, HID])
        xlT = sb("xlT", [128, BLOCK])
        sum_a = sb("sum_a", [128, BLOCK])
        gnn = sb("gnn", [128, BLOCK])
        rec = sb("rec", [TP, TILES, REC])
        x2 = sb("x2", [TP, TILES, HID])
        x2T = sb("x2T", [128, BLOCK])
        ones = sb("ones", [TP, TP])
        counts = sb("counts", [TP, EXPERTS])
        neghalf = sb("neghalf", [TP, TILES])
        quarters = sb("quarters", [TP, TILES])
        st = sb("st", [TP, TILES, 6])
        xst = sb("xst", [TP, TILES, 6])
        xw = sb("xw", [TP, TILES, 6])
        xrs = sb("xrs", [TP, TILES])
        xnb = sb("xnb", [TP, TILES])
        carrier_dve = sb("carrier_dve", [1, 1])
        w = sb("w", [TP, TILES, 6])
        carrier_pool = sb("carrier_pool", [TP, 3])
        lg = sb("lg", [TP, TILES, EXPERTS])
        lgm = sb("lgm", [TP, TILES, EXPERTS])
        mx = sb("mx", [TP, TILES])
        ex = sb("ex", [TP, TILES, EXPERTS])
        exs = sb("exs", [TP, TILES])
        wmask = sb("wmask", [TP, TILES, EXPERTS])
        best = sb("best", [TP, TILES])
        oh = sb("oh", [TP, TILES, EXPERTS])
        run = sb("run", [TP, TILES, EXPERTS])
        place = sb("place", [TP, TILES, EXPERTS])
        placed = sb("placed", [TP, TILES, EXPERTS])
        pos1 = sb("pos1", [TP, TILES])
        drop = sb("drop", [TP, TILES])
        slotf = sb("slotf", [TP, TILES])
        slot = sb("slot", [TP, TILES], U32)
        tok = sb("tok", [TP, 2, TILES])
        kept_out = sb("kept_out", [TP, TILES], U32)
        over = sb("over", [TP, TILES])
        cut = sb("cut", [TP, EXPERTS])
        used = sb("used", [RUNS, EXPERTS])
        clear_runs = sb("clear_runs", [RUNS, EXPERTS], U32)
        cut_of = sb("cut_of", [EDGE, EXPERTS])
        begun = sb("begun", [EDGE, RUNS])
        edge, runs_begun, edge_no, edge_slot, taken = (sb(name, [EDGE, 1]) for name in
                                                       ("edge", "runs_begun", "edge_no", "edge_slot", "taken"))
        clear_edge = sb("clear_edge", [EDGE, 1], U32)
        base = sb("base", [TP, TILES])
        wb1 = early[:, 0:2 * FF].rearrange("p (r n) -> p r n", r=2)
        wb2 = early[:, 2 * FF:2 * FF + 2 * W2].rearrange("p (r n) -> p r n", r=2)

        tail_at = [0]
        rawf = raw[:, :, :].rearrange("p r n -> p (r n)")

        def tail(rows, ring, *shape):
            n = 1
            for s in shape:
                n *= s
            a = tail_at[0]
            tail_at[0] += ring * n
            assert tail_at[0] <= RAW * GMAX * BLOCK
            v = rawf[0:rows, a:a + ring * n]
            if len(shape) == 1:
                return v.rearrange("p (r a) -> p r a", r=ring)
            return v.rearrange("p (r a b) -> p r a b", r=ring, a=shape[0])

        hm = tail(128, 2, FC, UNIT)
        recq = tail(SLOT_P, BODY, 4, REC)
        x2q = tail(SLOT_P, 2, 4, HID)
        x2q_hi, x2q_lo = (t[:, 0, 0:2 * UNIT].rearrange("p (r n) -> p r n", r=2) for t in (a_hi, a_lo))
        w1_hi, w1_lo = (t[:, 1, 0:2 * FF].rearrange("p (r n) -> p r n", r=2) for t in (a_hi, a_lo))
        yT = [t[:, 0:UNIT] for t in (x2T, xlT)]
        y = tail(SLOT_P, 1, 4, HID)
        ypos = xb[0:SLOT_P, :, :].rearrange("p j d -> p (j d)").unsqueeze(1)
        yneg = xl[0:SLOT_P, :, :].rearrange("p j d -> p (j d)").unsqueeze(1)
        ymask = x2[0:SLOT_P, :, :].rearrange("p j d -> p (j d)").unsqueeze(1)
        yout = tail(SLOT_P, 2, 4, HID)
        toki = sb("toki", [SLOT_P, BODY, 4], U32)

        bank = [ctx.enter_context(nc.psum_tensor(f"bank{i}", [128, 512], F32)) for i in range(8)]
        acc_a, acc_b, ps_gnn, ps_x, ps_g, ps_h0, ps_h1 = bank[:7]
        ps_logit = ps_g[0:TP, 0:TILES * EXPERTS].rearrange("p (j e) -> p j e", j=TILES)
        ps_count = bank[7][0:TP, 0:EXPERTS]
        ps_total = bank[7][0:TP, EXPERTS:2 * EXPERTS]
        ps_h = [ps_h0, ps_h1]
        ps_mid, ps_in, ps_y, ps_out = bank[0:4], bank[4], bank[5], bank[6]

        consts_loaded = sem("consts_loaded")
        zeros_set = sem("zeros_set")
        total_done = sem("total_done")
        clear_runs_ready = sem("clear_runs_ready")
        clear_edge_ready = sem("clear_edge_ready")
        runs_cleared = sem("runs_cleared")
        edges_cleared = sem("edges_cleared")
        scattered = sem("scattered")
        passed_on = sem("passed_on")
        rec_free = sem("rec_free")
        set_up = sem("set_up")
        items_loaded = [sem(f"items_loaded{i}") for i in range(2)]
        h_product = sem("h_product")
        h_biased = sem("h_biased")
        h_hi_ready = sem("h_hi_ready")
        h_lo_ready = sem("h_lo_ready")
        raw_loaded = [sem(f"raw_loaded{i}") for i in range(RAW)]
        hi_ready = sem("hi_ready")
        lo_ready = sem("lo_ready")
        multiplied = sem("multiplied")
        x_loaded = sem("x_loaded")
        x_stats = sem("x_stats")
        x_norm = sem("x_norm")
        xl_ready = sem("xl_ready")
        xl_turned = sem("xl_turned")
        xlT_ready = sem("xlT_ready")
        a_taken = sem("a_taken")
        gnn_ready = sem("gnn_ready")
        gnn_turned = sem("gnn_turned")
        x1_ready = sem("x1_ready")
        stats_ready = sem("stats_ready")
        norm_ready = sem("norm_ready")
        x2_ready = sem("x2_ready")
        x2_turned = sem("x2_turned")
        x2T_ready = sem("x2T_ready")
        logits_done = sem("logits_done")
        shifted = sem("shifted")
        exp_done = sem("exp_done")
        run_ready = sem("run_ready")
        count_done = sem("count_done")
        slots_ready = sem("slots_ready")
        dve_chain = sem("dve_chain")
        dve_unused_chain = sem("dve_unused_chain")
        pool_x_chain = sem("pool_x_chain")
        pool_x1_chain = sem("pool_x1_chain")
        weights_loaded = [sem(f"weights_loaded{i}") for i in range(2)]
        recq_loaded = [sem(f"recq_loaded{i}") for i in range(BODY)]
        x2q_ready = sem("x2q_ready")
        x2q_turned = sem("x2q_turned")
        x2q_hi_ready = sem("x2q_hi_ready")
        x2q_lo_ready = sem("x2q_lo_ready")
        w1_hi_ready = sem("w1_hi_ready")
        w1_lo_ready = sem("w1_lo_ready")
        mid_done = sem("mid_done")
        hm_ready = sem("hm_ready")
        y_done = sem("y_done")
        yT_ready = sem("yT_ready")
        y_turned = sem("y_turned")
        yout_ready = sem("yout_ready")
        y_gated = sem("y_gated")
        y_parts = sem("y_parts")
        toki_ready = sem("toki_ready")
        sent = [sem(f"sent{i}") for i in range(2)]

        class Chain:

            def __init__(self, eng, s, per):
                self.eng, self.s, self.per, self.n, self.base = eng, s, per, 0, 0

            def round(self, r):
                assert self.n in (0, self.per), (self.n, self.per)
                self.n, self.base = 0, r * self.per

            def did(self, ins):
                ins.then_inc(self.s, 1)
                self.n += 1

            def link(self, ins):
                self.did(ins)
                self.eng.wait_ge(self.s, self.base + self.n)

        def blocks(eng, body):
            body(0)
            with eng.Fori(1, BLOCKS) as b:
                body(b)

        def steps(eng, step):
            for k in range(BODY):
                step(0, k, k)
            with eng.Fori(1, UNITS // BODY) as i:
                for k in range(BODY):
                    step(i, k, None)
            for s in range(UNITS, UNITS + LAG_OUT):
                step(s // BODY, s % BODY, s)


        def has(at, lag):
            return at is None or 0 <= at - lag < UNITS

        def group_cols(g):
            return SIZES[g] * BLOCK

        def loads(b, g):
            extra = 1 if g % RAW == (GROUPS - 1) % RAW else 0
            return (b * (PER_RAW + extra) + g // RAW + 1 + (1 if g == GROUPS - 1 else 0)) * 16

        def wait_on_dve(dve, s, n):
            dve.wait_ge(s, n)
            nc.vector.memset(carrier_dve[:, :], 0.0)

        def wait_on_pool(pool, s, n, cell=0):
            pool.wait_ge(s, n)
            return nc.gpsimd.tensor_tensor(carrier_pool[:, cell:cell + 1], ones[:, 0:1], ones[:, 0:1], ALU.add)

        block = ctx.enter_context(nc.Block())

        @block.sync
        def _(sp):
            x_rows = x.rearrange("(r j) d -> r (j d)", j=TILES)
            parts = ((0, 112), (112, TP))

            def load_items(g):
                if g >= 2:
                    sp.wait_ge(h_product, g - 1)
                a = FIRST[g] * 128
                b = min(a + SIZES[g] * 128, ITEMS)
                sp.dma_start(items[:, g % 2, 0:b - a], items_t[:, a:b]).then_inc(items_loaded[g % 2], 16)

            def load_x(b):
                for lo, hi in parts:
                    sp.dma_start(xb[lo:hi, :, :].rearrange("p j d -> p (j d)"),
                                 x_rows[bass.ds(b * TP + lo, hi - lo), :]).then_inc(x_loaded, 16)

            def body(b):
                first = isinstance(b, int)
                for g in range(GROUPS):
                    if not first or g >= RAW:
                        sp.wait_ge(lo_ready, b * GROUPS + g - RAW + 1)
                    last = g == GROUPS - 1
                    n = (SIZES[g] - last) * BLOCK
                    a = FIRST[g] * BLOCK
                    adj_b = adj_m[b] if first else adj_m[bass.ds(b, 1), :, :].rearrange("o p n -> (o p) n")
                    sp.dma_start(raw[:, g % RAW, 0:n], adj_b[:, a:a + n],
                                 max_dma_last_dim=16384).then_inc(raw_loaded[g % RAW], 16)
                    if last:
                        rem_b = adj_r[b] if first else adj_r[bass.ds(b, 1), :, :].rearrange("o p n -> (o p) n")
                        sp.dma_start(raw[0:REM, g % RAW, n:n + BLOCK], rem_b).then_inc(raw_loaded[g % RAW], 16)
                    if first and g + 2 < GROUPS:
                        load_items(g + 2)
                    if first and g == 5:
                        load_x(b)
                    if not first and g == 9:
                        sp.wait_ge(x1_ready, b)
                        load_x(b)

            sp.dma_start(cst[:, :], consts).then_inc(consts_loaded, 16)
            load_items(0)
            load_items(1)
            blocks(sp, body)

            def load_weights(e, slot_, wait):
                if wait:
                    sp.wait_ge(yT_ready, (e - 1) * UNITS_E)
                w1_e = w1[bass.ds(e, 1), :, :].rearrange("o p n -> (o p) n")
                w2_e = w2[bass.ds(e, 1), :, :].rearrange("o p n -> (o p) n")
                sp.dma_start(wb1[:, slot_, :], w1_e).then_inc(weights_loaded[slot_], 16)
                sp.dma_start(wb2[:, slot_, :], w2_e).then_inc(weights_loaded[slot_], 16)

            rec_units = rec_d.rearrange("(r j) c -> r (j c)", j=4)

            def load_rec(q, k, wait):
                if wait:
                    sp.wait_ge(toki_ready, q - BODY + 1)
                    sp.wait_ge(yout_ready, q - BODY + 1)
                sp.dma_start(recq[:, k, :, :].rearrange("p j c -> p (j c)"),
                             rec_units[bass.ds(q * SLOT_P, SLOT_P), :]).then_inc(recq_loaded[k], 16)

            sp.wait_ge(edges_cleared, 16)
            sp.wait_ge(runs_cleared, EXPERTS * 16)
            load_weights(0, 0, False)
            sp.wait_ge(scattered, BLOCKS * TILES * 16)
            for k in range(BODY):
                if k == 2:
                    load_weights(1, 1, False)
                load_rec(k, k, False)
            with sp.Fori(1, UNITS // BODY) as i:
                for k in range(BODY):
                    if k % UNITS_E == 2:
                        load_weights(i * 2 + k // UNITS_E, k // UNITS_E, True)
                    load_rec(i * BODY + k, k, True)
            sp.wait_ge(passed_on, BLOCKS * TILES * 16)
            for k in range(2):
                sp.wait_ge(sent[k], UNITS // 2 * 64)

        @block.scalar
        def _(act):
            act.wait_ge(consts_loaded, 16)

            def h_high(g):
                act.wait_ge(h_biased, g + 1)
                a, n = FIRST[g] * HID, SIZES[g] * HID
                m = n - HID if g == GROUPS - 1 else n
                last = nc.scalar.copy(h_hi[:, a:a + m], h_raw[:, 0:m])
                if m < n:
                    last = nc.scalar.copy(h_hi[0:REM, a + m:a + n], h_raw[0:REM, m:n])
                last.then_inc(h_hi_ready, 1)

            def high(b, g):
                act.wait_ge(raw_loaded[g % RAW], loads(b, g))
                if not isinstance(b, int) or g >= HI_RING:
                    act.wait_ge(multiplied, b * GROUPS + g - HI_RING + 1)
                m = group_cols(g)
                nc.scalar.copy(a_hi[:, g % HI_RING, 0:m], raw[:, g % RAW, 0:m]).then_inc(hi_ready, 1)

            def take_a(b):
                act.wait_ge(multiplied, b * GROUPS + HALF)
                if not isinstance(b, int):
                    act.wait_ge(gnn_ready, b)
                nc.scalar.activation(sum_a[:, :], acc_a[:, 0:BLOCK], ACT.Identity,
                                     bias=const("b_user")).then_inc(a_taken, 1)

            def normalize_x(b):
                act.wait_ge(x_norm, b + 1)
                if not isinstance(b, int):
                    act.wait_ge(xl_turned, b)
                for j in range(TILES):
                    last = nc.scalar.activation(xl[:, j, :], xb[:, j, :], ACT.Identity,
                                                scale=xrs[:, j:j + 1], bias=xnb[:, j:j + 1])
                last.then_inc(xl_ready, 1)

            def take_xl(b):
                act.wait_ge(xl_turned, b + 1)
                if not isinstance(b, int):
                    act.wait_ge(multiplied, b * GROUPS)
                nc.scalar.copy(xlT[:, :], ps_x[:, 0:BLOCK]).then_inc(xlT_ready, 1)

            def normalize_x1(n):
                act.wait_ge(norm_ready, n + 1)
                for j in range(TILES):
                    last = nc.scalar.activation(x2[:, j, :], rec[:, j, 0:HID], ACT.Identity,
                                                scale=rec[:, j, C_RSTD:C_RSTD + 1],
                                                bias=rec[:, j, C_NB:C_NB + 1])
                last.then_inc(x2_ready, 1)

            def take_x2(n):
                act.wait_ge(x2_turned, n + 1)
                nc.scalar.copy(x2T[:, :], ps_x[:, 0:BLOCK]).then_inc(x2T_ready, 1)

            def exps(n):
                act.wait_ge(shifted, n + 1)
                nc.scalar.activation(ex[:, :, :], lgm[:, :, :], ACT.Exp).then_inc(exp_done, 1)

            def body(b):
                first = isinstance(b, int)
                for g in range(GROUPS):
                    high(b, g)
                    if first and g + 1 < GROUPS:
                        h_high(g + 1)
                    if not first:
                        {7: normalize_x1, 9: take_x2, 12: exps}.get(g, lambda n: None)(b - 1)
                    {14: normalize_x, 15: take_a, 17: take_xl}.get(g, lambda b: None)(b)

            h_high(0)
            blocks(act, body)
            normalize_x1(BLOCKS - 1)
            take_x2(BLOCKS - 1)
            exps(BLOCKS - 1)

            def bias_of(k, lag, col):
                return wb2[:, (k - lag) // UNITS_E % 2, FC * HID + col:FC * HID + col + 1]

            def step(i, k, at):
                s = i * BODY + k
                if has(at, 0) and k % UNITS_E == 0:
                    e = i * 2 + k // UNITS_E
                    act.wait_ge(weights_loaded[k // UNITS_E], (i + 1) * 32)
                    if at is None:
                        act.wait_ge(mid_done, (e - 1) * (UNITS_E * FC))
                    nc.scalar.copy(w1_hi[:, k // UNITS_E, :], wb1[:, k // UNITS_E, :]).then_inc(w1_hi_ready, 1)
                if has(at, LAG_IN):
                    act.wait_ge(x2q_turned, s)
                    if at is None or at - LAG_IN >= 2:
                        act.wait_ge(mid_done, (s - 2) * FC)
                    nc.scalar.copy(x2q_hi[:, (k - LAG_IN) % 2, :], ps_in[:, 0:UNIT]).then_inc(x2q_hi_ready, 1)
                if has(at, 0):
                    act.wait_ge(recq_loaded[k], (i + 1) * 16)
                    if at is None or at >= 2:
                        act.wait_ge(x2q_turned, s - 1)
                    for j in range(4):
                        last = nc.scalar.activation(x2q[:, k % 2, j, :], recq[:, k, j, 0:HID], ACT.Identity,
                                                    scale=recq[:, k, j, C_RSTD:C_RSTD + 1],
                                                    bias=recq[:, k, j, C_NB:C_NB + 1])
                    last.then_inc(x2q_ready, 1)
                if has(at, LAG_MID):
                    if at is None or at - LAG_MID >= 2:
                        act.wait_ge(y_done, s - 3)
                    for f in range(FC):
                        act.wait_ge(mid_done, (s - 2) * FC + f + 1)
                        nc.scalar.activation(hm[:, (k - LAG_MID) % 2, f, :], ps_mid[f][:, 0:UNIT], ACT.Relu,
                                             bias=bias_of(k, LAG_MID, f)).then_inc(hm_ready, 1)
                if has(at, LAG_Y):
                    act.wait_ge(y_done, s - 2)
                    if at is None or at - LAG_Y >= 2:
                        act.wait_ge(y_turned, s - 4)
                    nc.scalar.activation(yT[(k - LAG_Y) % 2], ps_y[:, 0:UNIT], ACT.Identity,
                                         bias=bias_of(k, LAG_Y, FC)).then_inc(yT_ready, 1)

            steps(act, step)

        @block.vector
        def _(dve):
            v = nc.vector
            chain = Chain(dve, dve_chain, 21)
            unused_chain = Chain(dve, dve_unused_chain, 9)
            rev = const("rev", TP).rearrange("p (j e) -> p j e", j=TILES)
            gate_b = const("gate_b", TP).rearrange("p (j e) -> p j e", j=TILES)

            def each(t):
                return t[:, :].unsqueeze(2).broadcast_to([TP, TILES, EXPERTS])

            def h_bias(g):
                dve.wait_ge(h_product, g + 1)
                if g >= 1:
                    dve.wait_ge(h_lo_ready, g)
                n = SIZES[g]
                m = n - 1 if g == GROUPS - 1 else n
                last = v.tensor_tensor(h_raw[:, 0:m * HID].rearrange("p (c d) -> p c d", d=HID),
                                       ps_h[g % 2][:, 0:m * HID].rearrange("p (c d) -> p c d", d=HID),
                                       const("b_item").unsqueeze(1).broadcast_to([128, m, HID]), ALU.add)
                if m < n:
                    last = v.tensor_tensor(h_raw[0:REM, m * HID:n * HID], ps_h[g % 2][0:REM, m * HID:n * HID],
                                           const("b_item", REM), ALU.add)
                last.then_inc(h_biased, 1)

            def h_low(g):
                dve.wait_ge(h_hi_ready, g + 1)
                a, n = FIRST[g] * HID, SIZES[g] * HID
                m = n - HID if g == GROUPS - 1 else n
                last = v.tensor_tensor(h_lo[:, a:a + m], h_raw[:, 0:m], h_hi[:, a:a + m].bitcast(F32), ALU.subtract)
                if m < n:
                    last = v.tensor_tensor(h_lo[0:REM, a + m:a + n], h_raw[0:REM, m:n],
                                           h_hi[0:REM, a + m:a + n].bitcast(F32), ALU.subtract)
                last.then_inc(h_lo_ready, 1)

            def low(b, g):
                dve.wait_ge(hi_ready, b * GROUPS + g + 1)
                if not isinstance(b, int) or g >= LO_RING:
                    dve.wait_ge(multiplied, b * GROUPS + g - LO_RING + 1)
                m = group_cols(g)
                v.tensor_tensor(a_lo[:, g % LO_RING, 0:m], raw[:, g % RAW, 0:m],
                                a_hi[:, g % HI_RING, 0:m].bitcast(F32), ALU.subtract).then_inc(lo_ready, 1)

            def x_statistics(b):
                dve.wait_ge(x_loaded, 32 * (b + 1))
                if not isinstance(b, int):
                    dve.wait_ge(x_norm, b)
                for j in range(TILES):
                    last = v.bn_stats(xst[:, j, :], xb[:, j, :])
                last.then_inc(x_stats, 1)

            def sum_gnn(n):
                dve.wait_ge(multiplied, (n + 1) * GROUPS)
                dve.wait_ge(a_taken, n + 1)
                v.tensor_tensor(gnn[:, :], acc_b[:, 0:BLOCK], sum_a[:, :], ALU.add).then_inc(gnn_ready, 1)

            def add_x(n):
                chain.round(n)
                dve.wait_ge(gnn_turned, n + 1)
                dve.wait_ge(rec_free, n + 1)
                v.scalar_tensor_tensor(out=rec[:, :, 0:HID],
                                       in0=ps_gnn[0:TP, :].rearrange("p (j d) -> p j d", j=TILES), scalar=0.0,
                                       in1=xb[:, :, :], op0=ALU.max, op1=ALU.add).then_inc(x1_ready, 1)
                dve.wait_ge(x1_ready, n + 1)
                for j in range(TILES):
                    last = v.bn_stats(st[:, j, :], rec[:, j, 0:HID])
                last.then_inc(stats_ready, 1)

            def choose(n):
                dve.wait_ge(logits_done, n + 1)
                chain.link(v.tensor_tensor(lg[:, :, :], ps_logit, gate_b, ALU.add))
                chain.did(v.tensor_scalar(tok[:, :, :], tok[:, :, :], float(BLOCK), None, ALU.add))
                chain.link(v.tensor_reduce(mx[:, :], lg[:, :, :], AX.X, ALU.max))
                v.tensor_tensor(lgm[:, :, :], lg[:, :, :], each(mx), ALU.subtract).then_inc(shifted, 1)
                dve.wait_ge(shifted, n + 1)
                chain.link(v.scalar_tensor_tensor(out=wmask[:, :, :], in0=lgm[:, :, :], scalar=0.0, in1=rev,
                                                  op0=ALU.is_ge, op1=ALU.mult))
                chain.link(v.tensor_reduce(best[:, :], wmask[:, :, :], AX.X, ALU.max))
                chain.link(v.tensor_tensor(oh[:, :, :], rev, each(best), ALU.is_equal))
                chain.did(v.tensor_copy(run[:, 0, :], oh[:, 0, :]))
                chain.link(v.tensor_tensor(run[:, 1, :], oh[:, 0, :], oh[:, 1, :], ALU.add))
                chain.link(v.tensor_tensor(run[:, 2, :], run[:, 1, :], oh[:, 2, :], ALU.add))
                v.tensor_tensor(run[:, 3, :], run[:, 2, :], oh[:, 3, :], ALU.add).then_inc(run_ready, 1)

            def find_unused(n):
                dve.wait_ge(total_done, n + 1)
                unused_chain.round(n)
                unused_chain.link(v.tensor_scalar(cut[:, :], ps_total, float(CAP), None, ALU.min))
                unused_chain.did(v.tensor_scalar(used[:, :], cut[0:RUNS, :], const("run_at", RUNS), BEYOND,
                                                 ALU.is_gt, ALU.mult))
                unused_chain.link(v.tensor_tensor(cut_of[:, :], cut[0:EDGE, :], const("edge_of", EDGE), ALU.mult))
                unused_chain.link(v.tensor_reduce(edge[:, :], cut_of[:, :], AX.X, ALU.add))
                v.tensor_tensor(clear_runs[:, :], used[:, :], const("run_no", RUNS),
                                ALU.add).then_inc(clear_runs_ready, 1)

            def find_edges(n):
                unused_chain.link(v.tensor_scalar(begun[:, :], const("starts", EDGE), edge[:, :], None, ALU.is_lt))
                unused_chain.link(v.tensor_reduce(runs_begun[:, :], begun[:, :], AX.X, ALU.add))
                unused_chain.did(v.tensor_scalar(edge_no[:, :], runs_begun[:, :], float(RUN), const("edge_no", EDGE),
                                                 ALU.mult, ALU.add))
                unused_chain.link(v.tensor_scalar(edge_slot[:, :], runs_begun[:, :], float(RUN),
                                                  const("edge_at", EDGE), ALU.mult, ALU.add))
                unused_chain.link(v.tensor_tensor(taken[:, :], edge[:, :], edge_no[:, :], ALU.is_gt))
                v.scalar_tensor_tensor(out=clear_edge[:, :], in0=taken[:, :], scalar=BEYOND,
                                       in1=edge_slot[:, :], op0=ALU.mult, op1=ALU.add).then_inc(clear_edge_ready, 1)

            def assign(n):
                dve.wait_ge(count_done, n + 1)
                dve.wait_ge(run_ready, n + 1)
                chain.link(v.tensor_tensor(place[:, :, :], run[:, :, :],
                                           ps_count.unsqueeze(1).broadcast_to([TP, TILES, EXPERTS]), ALU.add))
                chain.link(v.tensor_tensor(placed[:, :, :], place[:, :, :], oh[:, :, :], ALU.mult))
                chain.link(v.tensor_reduce(pos1[:, :], placed[:, :, :], AX.X, ALU.add))
                chain.did(v.tensor_scalar(over[:, :], pos1[:, :], float(CAP), None, ALU.is_gt))
                chain.did(v.tensor_scalar(base[:, :], best[:, :], -float(SLOTS_E), float(SLOTS - 1),
                                          ALU.mult, ALU.add))
                chain.did(v.tensor_tensor(counts[:, :], counts[:, :], run[:, 3, :], ALU.add))
                dve.wait_ge(exp_done, n + 1)
                chain.did(v.tensor_reduce(exs[:, :], ex[:, :, :], AX.X, ALU.add))
                chain.link(v.tensor_copy(rec[:, :, C_TOK:C_TOK + 1], tok[:, 0, :].unsqueeze(2)))
                chain.did(v.scalar_tensor_tensor(out=drop[:, :], in0=pos1[:, :], scalar=0.5, in1=over[:, :],
                                                 op0=ALU.is_lt, op1=ALU.max))
                chain.did(v.tensor_tensor(slotf[:, :], base[:, :], pos1[:, :], ALU.add))
                chain.link(v.reciprocal(rec[:, :, C_GATE:C_GATE + 1], exs[:, :].unsqueeze(2)))
                chain.did(v.scalar_tensor_tensor(out=kept_out[:, :], in0=drop[:, :], scalar=-BEYOND,
                                                 in1=tok[:, 1, :], op0=ALU.mult, op1=ALU.add))
                v.scalar_tensor_tensor(out=slot[:, :], in0=drop[:, :], scalar=BEYOND,
                                       in1=slotf[:, :], op0=ALU.mult, op1=ALU.add).then_inc(slots_ready, 1)

            def body(b):
                first = isinstance(b, int)
                for g in range(GROUPS):
                    low(b, g)
                    if first and g + 1 < GROUPS:
                        h_low(g + 1)
                    if first and g + 2 < GROUPS:
                        h_bias(g + 2)
                    if not first:
                        {2: sum_gnn, 4: add_x, 10: choose, 12: find_unused, 13: assign,
                         15: find_edges}.get(g, lambda n: None)(b - 1)
                    if g == 11:
                        x_statistics(b)

            v.memset(rec[:, :, :], 0.0).then_inc(rec_free, 1)
            v.memset(ones[:, :], 1.0).then_inc(set_up, 1)
            v.memset(counts[:, :], 0.0).then_inc(set_up, 1)
            v.memset(neghalf[:, :], -0.5).then_inc(set_up, 1)
            v.memset(quarters[:, :], 0.25).then_inc(set_up, 1)
            dve.wait_ge(consts_loaded, 16)
            v.tensor_copy(tok[:, :, :].rearrange("p a j -> p (a j)"), const("tok", TP)).then_inc(set_up, 1)
            dve.wait_ge(set_up, 5)
            h_bias(0)
            h_low(0)
            h_bias(1)
            blocks(dve, body)
            for stage in (sum_gnn, add_x, choose, assign):
                stage(BLOCKS - 1)

            def step(i, k, at):
                s = i * BODY + k
                if has(at, 0) and k % UNITS_E == 0:
                    e = k // UNITS_E
                    dve.wait_ge(w1_hi_ready, i * 2 + e + 1)
                    v.tensor_tensor(w1_lo[:, e, :], wb1[:, e, :], w1_hi[:, e, :].bitcast(F32),
                                    ALU.subtract).then_inc(w1_lo_ready, 1)
                if has(at, LAG_IN):
                    u = (k - LAG_IN) % 2
                    dve.wait_ge(x2q_hi_ready, s)
                    v.tensor_tensor(x2q_lo[:, u, :], ps_in[:, 0:UNIT], x2q_hi[:, u, :].bitcast(F32),
                                    ALU.subtract).then_inc(x2q_lo_ready, 1)
                if has(at, LAG_OUT):
                    u, r = (k - LAG_OUT) % 2, (k - LAG_OUT) % BODY
                    n = s - LAG_OUT
                    dve.wait_ge(y_turned, n + 1)
                    yf = y[:, 0, :, :].rearrange("p j d -> p (j d)")
                    if at is None or at > LAG_OUT:
                        dve.wait_ge(yout_ready, n)
                    v.tensor_tensor(y[:, 0, :, :], ps_out[0:SLOT_P, :].rearrange("p (j d) -> p j d", j=4),
                                    recq[:, r, :, C_GATE:C_GATE + 1].broadcast_to([SLOT_P, 4, HID]),
                                    ALU.mult).then_inc(y_gated, 1)
                    dve.wait_ge(y_gated, n + 1)
                    v.tensor_scalar(ypos[:, 0, :], yf, 0.0, CLIP, ALU.max, ALU.min)
                    v.tensor_scalar(yneg[:, 0, :], yf, 0.0, -CLIP, ALU.min, ALU.max)
                    v.tensor_scalar(ymask[:, 0, :].bitcast(U32), yf, 0.0, 0.0, ALU.mult,
                                    ALU.not_equal).then_inc(y_parts, 1)
                    dve.wait_ge(y_parts, n * 3 + 1)
                    v.tensor_tensor(ypos[:, 0, :], ypos[:, 0, :], yneg[:, 0, :], ALU.add).then_inc(y_parts, 1)
                    wait_on_dve(dve, y_parts, n * 3 + 2)
                    v.copy_predicated(yf, ymask[:, 0, :].bitcast(U32), ypos[:, 0, :]).then_inc(y_parts, 1)
                    dve.wait_ge(y_parts, n * 3 + 3)
                    if at is None or at - LAG_OUT >= 2:
                        dve.wait_ge(sent[u], (i * (BODY // 2) + (k - LAG_OUT) // 2) * 64)
                    v.tensor_tensor(yout[:, u, :, :], y[:, 0, :, :], recq[:, r, :, 0:HID],
                                    ALU.add).then_inc(yout_ready, 1)

            steps(dve, step)

        @block.gpsimd
        def _(pool):
            p = nc.gpsimd
            def norm(sums, w, rstd, nb, chain, done):
                def cell(k):
                    return w[:, :, k:k + 1]

                total, diff, sq, diff2, quarter, var = map(cell, range(6))
                chain.did(p.tensor_tensor(total, sums[:, :, 1:2], sums[:, :, 4:5], ALU.add))
                chain.did(p.tensor_tensor(diff, sums[:, :, 1:2], sums[:, :, 4:5], ALU.subtract))
                chain.link(p.tensor_tensor(sq, sums[:, :, 2:3], sums[:, :, 5:6], ALU.add))
                chain.did(p.tensor_tensor(diff2, diff, diff, ALU.mult))
                chain.did(p.tensor_scalar(total, total, -0.5, None, ALU.mult))
                chain.link(p.tensor_scalar(sq, sq, 1.0 / HID, EPS, ALU.mult, ALU.add))
                chain.link(p.tensor_tensor(quarter, diff2, quarters[:, :].unsqueeze(2), ALU.mult))
                chain.link(p.tensor_tensor(var, quarter, sq, ALU.add))
                chain.link(p.tensor_tensor(rstd, var, neghalf[:, :].unsqueeze(2), ALU.pow))
                p.tensor_tensor(nb, total, rstd, ALU.mult).then_inc(done, 1)

            x_chain = Chain(pool, pool_x_chain, 9)
            x1_chain = Chain(pool, pool_x1_chain, 9)

            def norm_x(b):
                x_chain.round(b)
                if not isinstance(b, int):
                    pool.wait_ge(xl_ready, b)
                pool.wait_ge(x_stats, b + 1)
                norm(xst, xw, xrs[:, :].unsqueeze(2), xnb[:, :].unsqueeze(2), x_chain, x_norm)

            def norm_x1(n):
                x1_chain.round(n)
                pool.wait_ge(stats_ready, n + 1)
                norm(st, w, rec[:, :, C_RSTD:C_RSTD + 1], rec[:, :, C_NB:C_NB + 1], x1_chain, norm_ready)

            def scatter(n):
                wait_on_pool(pool, slots_ready, n + 1)
                for j in range(TILES):
                    p.indirect_dma_start(rec_d, bass.IndirectOffsetOnAxis(ap=slot[:, j:j + 1], axis=0),
                                         rec[:, j, :], None, bounds_check=SLOTS - 1,
                                         oob_is_err=False).then_inc(scattered, 16)
                for j in range(TILES):
                    p.indirect_dma_start(out, bass.IndirectOffsetOnAxis(ap=kept_out[:, j:j + 1], axis=0),
                                         rec[:, j, 0:HID], None, bounds_check=USERS - 1,
                                         oob_is_err=False).then_inc(passed_on, 16)

            def sent_off(n):
                pool.wait_ge(passed_on, (n + 1) * (TILES * 16))
                wait_on_pool(pool, scattered, (n + 1) * (TILES * 16), 1).then_inc(rec_free, 1)

            def set_zeros():
                pool.wait_ge(h_lo_ready, GROUPS)
                p.memset(zeros[0:TP, :], 0.0).then_inc(zeros_set, 1)
                pool.wait_ge(zeros_set, 1)

            def clear_edges():
                pool.wait_ge(clear_edge_ready, BLOCKS - 1)
                p.indirect_dma_start(rec_d, bass.IndirectOffsetOnAxis(ap=clear_edge[:, :], axis=0),
                                     zeros[0:EDGE, 0:REC], None, bounds_check=SLOTS - 1,
                                     oob_is_err=False).then_inc(edges_cleared, 16)

            def clear_slots(experts):
                pool.wait_ge(clear_runs_ready, BLOCKS - 1)
                for e in experts:
                    p.indirect_dma_start(rec_d.rearrange("(n r) c -> n (r c)", r=RUN),
                                         bass.IndirectOffsetOnAxis(ap=clear_runs[:, e:e + 1], axis=0),
                                         zeros[0:RUNS, :], None, bounds_check=SLOTS // RUN - 1,
                                         oob_is_err=False).then_inc(runs_cleared, 16)

            pool.wait_ge(set_up, 5)
            norm_x(0)
            with pool.Fori(1, BLOCKS - 1) as b:
                norm_x1(b - 1)
                norm_x(b)
                scatter(b - 1)
                sent_off(b - 1)
            norm_x1(BLOCKS - 2)
            norm_x(BLOCKS - 1)
            set_zeros()
            scatter(BLOCKS - 2)
            clear_edges()
            clear_slots(range(EXPERTS // 2))
            sent_off(BLOCKS - 2)
            clear_slots(range(EXPERTS // 2, EXPERTS))
            norm_x1(BLOCKS - 1)
            pool.wait_ge(edges_cleared, 16)
            pool.wait_ge(runs_cleared, EXPERTS * 16)
            scatter(BLOCKS - 1)

            def step(i, k, at):
                n = i * BODY + (k - LAG_OUT)
                if has(at, LAG_OUT):
                    pool.wait_ge(toki_ready, n + 1)
                    pool.wait_ge(yout_ready, n + 1)
                if has(at, LAG_OUT - 1):
                    r = (k - LAG_OUT + 1) % BODY
                    wait_on_pool(pool, recq_loaded[r], (i + (k - LAG_OUT + 1) // BODY + 1) * 16, 2)
                    p.tensor_scalar(toki[:, r, :].unsqueeze(2), recq[:, r, :, C_TOK:C_TOK + 1],
                                    float(NO_TOKEN), None, ALU.add).then_inc(toki_ready, 1)
                if has(at, LAG_OUT):
                    for j in range(4):
                        p.indirect_dma_start(out, bass.IndirectOffsetOnAxis(
                            ap=toki[:, (k - LAG_OUT) % BODY, j:j + 1], axis=0),
                            yout[:, (k - LAG_OUT) % 2, j, :], None, bounds_check=USERS - 1,
                            oob_is_err=False).then_inc(sent[(k - LAG_OUT) % 2], 16)

            steps(pool, step)

        @block.tensor
        def _(pe):
            def h_chunks(g):
                pe.wait_ge(items_loaded[g % 2], 16 * (g // 2 + 1))
                if g >= 2:
                    pe.wait_ge(h_biased, g - 1)
                for c in range(SIZES[g]):
                    m = REM if FIRST[g] + c == FULL else 128
                    last = nc.tensor.matmul(ps_h[g % 2][0:m, c * HID:(c + 1) * HID],
                                            items[:, g % 2, c * 128:c * 128 + m], const("w_item"),
                                            start=True, stop=True)
                last.then_inc(h_product, 1)

            def group(b, g):
                first = isinstance(b, int)
                acc = (acc_a if g < HALF else acc_b)[:, 0:BLOCK]
                if first:
                    pe.wait_ge(h_hi_ready, g + 1)
                    pe.wait_ge(h_lo_ready, g + 1)
                elif g == 0:
                    pe.wait_ge(a_taken, b)
                elif g == HALF:
                    pe.wait_ge(gnn_ready, b)
                pe.wait_ge(hi_ready, b * GROUPS + g + 1)
                for part in range(2):
                    if part:
                        pe.wait_ge(lo_ready, b * GROUPS + g + 1)
                    for c in range(SIZES[g]):
                        m = REM if FIRST[g] + c == FULL else 128
                        k = FIRST[g] + c
                        opens = g in (0, HALF) and c == 0 and part == 0
                        closes = g in (HALF - 1, GROUPS - 1) and c == SIZES[g] - 1 and part == 1
                        h_high, h_low = h_hi[0:m, k * HID:(k + 1) * HID], h_lo[0:m, k * HID:(k + 1) * HID]
                        a = a_lo[0:m, g % LO_RING] if part else a_hi[0:m, g % HI_RING]
                        a = a[:, c * BLOCK:(c + 1) * BLOCK]
                        last = nc.tensor.matmul(acc, h_high, a, start=opens, stop=closes)
                        if not part:
                            nc.tensor.matmul(acc, h_low, a, start=False, stop=False)
                last.then_inc(multiplied, 1)

            def turn_x(b):
                pe.wait_ge(xl_ready, b + 1)
                if not isinstance(b, int):
                    pe.wait_ge(x2T_ready, b)
                for j in range(TILES):
                    last = nc.tensor.transpose(ps_x[:, j * TP:(j + 1) * TP], xl[:, j, :], ident[0:TP, 0:TP])
                last.then_inc(xl_turned, 1)

            def users(b):
                pe.wait_ge(xlT_ready, b + 1)
                nc.tensor.matmul(acc_b[:, 0:BLOCK], const("w_user"), xlT[:, :], start=False, stop=False)

            def turn_gnn(n):
                pe.wait_ge(gnn_ready, n + 1)
                for j in range(TILES):
                    last = nc.tensor.transpose(ps_gnn[0:TP, j * HID:(j + 1) * HID], gnn[:, j * TP:(j + 1) * TP],
                                               ident)
                last.then_inc(gnn_turned, 1)

            def turn_x2(n):
                pe.wait_ge(x2_ready, n + 1)
                pe.wait_ge(xlT_ready, n + 1)
                for j in range(TILES):
                    last = nc.tensor.transpose(ps_x[:, j * TP:(j + 1) * TP], x2[:, j, :], ident[0:TP, 0:TP])
                last.then_inc(x2_turned, 1)

            def logits(n):
                pe.wait_ge(x2T_ready, n + 1)
                for j in range(TILES):
                    last = nc.tensor.matmul(ps_logit[:, j, :], x2T[:, j * TP:(j + 1) * TP], const("gate_w"),
                                            start=True, stop=True)
                last.then_inc(logits_done, 1)

            def count(n):
                pe.wait_ge(run_ready, n + 1)
                nc.tensor.matmul(ps_count, const("tri", TP), run[:, 3, :], start=True, stop=False)
                nc.tensor.matmul(ps_count, ones[:, :], counts[:, :], start=False, stop=True).then_inc(count_done, 1)

            def total(n):
                nc.tensor.matmul(ps_total, ones[:, :], run[:, 3, :], start=True, stop=False)
                nc.tensor.matmul(ps_total, ones[:, :], counts[:, :], start=False, stop=True).then_inc(total_done, 1)

            def body(b):
                first = isinstance(b, int)
                for g in range(GROUPS):
                    if first and g + 2 < GROUPS:
                        h_chunks(g + 2)
                    group(b, g)
                    if not first:
                        {2: turn_gnn, 7: turn_x2, 9: logits, 10: count}.get(g, lambda n: None)(b - 1)
                    if not first and g == 10:
                        total(b - 1)
                    {14: turn_x, 17: users}.get(g, lambda b: None)(b)

            pe.wait_ge(consts_loaded, 16)
            pe.wait_ge(set_up, 5)
            h_chunks(0)
            h_chunks(1)
            blocks(pe, body)
            for stage in (turn_gnn, turn_x2, logits, count):
                stage(BLOCKS - 1)

            def step(i, k, at):
                s = i * BODY + k
                if has(at, LAG_IN):
                    pe.wait_ge(x2q_ready, s)
                    if at is None or at > LAG_IN:
                        pe.wait_ge(x2q_lo_ready, s - 1)
                    for j in range(4):
                        last = nc.tensor.transpose(ps_in[:, j * SLOT_P:(j + 1) * SLOT_P],
                                                   x2q[:, (k - LAG_IN) % 2, j, :], ident[0:SLOT_P, 0:SLOT_P])
                    last.then_inc(x2q_turned, 1)
                if has(at, LAG_OUT):
                    pe.wait_ge(yT_ready, s - LAG_OUT + 1)
                    if at is None or at > LAG_OUT:
                        pe.wait_ge(y_gated, s - LAG_OUT)
                    for j in range(4):
                        last = nc.tensor.transpose(ps_out[0:SLOT_P, j * HID:(j + 1) * HID],
                                                   yT[(k - LAG_OUT) % 2][:, j * SLOT_P:(j + 1) * SLOT_P], ident)
                    last.then_inc(y_turned, 1)
                if has(at, LAG_MID):
                    w, u = (k - LAG_MID) // UNITS_E % 2, (k - LAG_MID) % 2
                    pe.wait_ge(w1_lo_ready, i * 2 + (k - LAG_MID) // UNITS_E + 1)
                    pe.wait_ge(x2q_lo_ready, s - 1)
                    for f in range(FC):
                        if at is None or at > LAG_MID:
                            pe.wait_ge(hm_ready, (s - 3) * FC + f + 1)
                        cols = slice(f * 128, (f + 1) * 128)
                        mid = ps_mid[f][:, 0:UNIT]
                        nc.tensor.matmul(mid, w1_hi[:, w, cols], x2q_hi[:, u, :], start=True, stop=False)
                        nc.tensor.matmul(mid, w1_lo[:, w, cols], x2q_hi[:, u, :], start=False, stop=False)
                        nc.tensor.matmul(mid, w1_hi[:, w, cols], x2q_lo[:, u, :], start=False,
                                         stop=True).then_inc(mid_done, 1)
                if has(at, LAG_Y):
                    w = (k - LAG_Y) // UNITS_E % 2
                    pe.wait_ge(weights_loaded[w], (i + (k - LAG_Y) // BODY + 1) * 32)
                    pe.wait_ge(hm_ready, (s - 2) * FC)
                    if at is None or at > LAG_Y:
                        pe.wait_ge(yT_ready, s - 3)
                    for f in range(FC):
                        last = nc.tensor.matmul(ps_y[:, 0:UNIT], wb2[:, w, f * HID:(f + 1) * HID],
                                                hm[:, (k - LAG_Y) % 2, f, :], start=(f == 0), stop=(f == FC - 1))
                    last.then_inc(y_done, 1)

            steps(pe, step)


def kernel(x, adj, L0_gnn_item_feat, L0_gnn_W_item, L0_gnn_b_item, L0_gnn_W_user, L0_gnn_b_user,
           L0_ffn_gate_w, L0_ffn_gate_b, L0_ffn_w1, L0_ffn_b1, L0_ffn_w2, L0_ffn_b2):
    import numpy as np
    import concourse.bacc as bacc
    from concourse.bass_utils import run_bass_kernel_spmd

    adj_t = np.asarray(adj).reshape(BLOCKS, TP, TILES, ITEMS).transpose(0, 3, 2, 1)
    adj_m = np.ascontiguousarray(
        adj_t[:, :FULL * 128].reshape(BLOCKS, FULL, 128, TILES, TP).transpose(0, 2, 1, 3, 4)
    ).reshape(BLOCKS, 128, FULL * BLOCK)
    adj_r = np.ascontiguousarray(adj_t[:, FULL * 128:]).reshape(BLOCKS, REM, BLOCK)

    consts = np.zeros((128, NCONST), np.float32)

    def put(name, a):
        lo, hi = COLS[name]
        consts[:a.shape[0], lo:hi] = a

    q = np.arange(TP)
    put("ident", np.eye(128, dtype=np.float32))
    put("tri", (q[:, None] < q[None, :]).astype(np.float32))
    put("rev", np.tile((EXPERTS - np.arange(EXPERTS)).astype(np.float32), (TP, TILES)))
    tok = q[:, None] * TILES + np.arange(TILES)[None, :] - BLOCK
    put("tok", np.concatenate([tok - NO_TOKEN, tok + BEYOND], axis=1).astype(np.float32))
    put("w_item", np.asarray(L0_gnn_W_item).T)
    put("w_user", np.asarray(L0_gnn_W_user).T)
    put("b_item", np.tile(np.asarray(L0_gnn_b_item), (128, 1)))
    put("gate_w", np.asarray(L0_ffn_gate_w))
    put("gate_b", np.tile(np.asarray(L0_ffn_gate_b), (TP, TILES)))
    e = np.arange(EXPERTS)
    put("run_at", (np.arange(RUNS) * RUN).astype(np.float32)[:, None])
    put("run_no", (e[None, :] * (SLOTS_E // RUN) + np.arange(RUNS)[:, None]).astype(np.float32))
    r = np.arange(EDGE)
    put("edge_of", (r[:, None] // RUN == e[None, :]).astype(np.float32))
    put("starts", np.tile((np.arange(RUNS) * RUN).astype(np.float32), (EDGE, 1)))
    put("edge_no", (r % RUN - RUN).astype(np.float32)[:, None])
    put("edge_at", (r // RUN * SLOTS_E + r % RUN - RUN).astype(np.float32)[:, None])
    put("b_user", np.asarray(L0_gnn_b_user).reshape(HID, 1))

    arrays = {
        "adj_m": adj_m,
        "adj_r": adj_r,
        "items_t": np.ascontiguousarray(np.asarray(L0_gnn_item_feat).T),
        "x": np.ascontiguousarray(np.asarray(x)),
        "consts": consts,
        "w1": np.ascontiguousarray(np.asarray(L0_ffn_w1)),
        "w2": np.concatenate([
            np.asarray(L0_ffn_w2).reshape(EXPERTS, FC, 128, HID).transpose(0, 2, 1, 3).reshape(EXPERTS, 128, FC * HID),
            np.asarray(L0_ffn_b1).reshape(EXPERTS, FC, 128).transpose(0, 2, 1),
            np.asarray(L0_ffn_b2).reshape(EXPERTS, HID, 1)], axis=2),
    }
    nc = bacc.Bacc("TRN2", target_bir_lowering=False, num_devices=1)
    aps = [nc.dram_tensor(name, a.shape, mybir.dt.from_np(a.dtype), kind="ExternalInput").ap()
           for name, a in arrays.items()]
    rec_d = nc.dram_tensor("records", (SLOTS, REC), F32, kind="Internal").ap()
    out = nc.dram_tensor("out", (USERS, HID), F32, kind="ExternalOutput").ap()
    build(nc, *aps, rec_d, out)
    r = run_bass_kernel_spmd(nc, [arrays], core_ids=[0])
    return r.results[0]["out"]
```
